# Optimizing a Trainium2 kernel written in Bass

```python
import numpy as np
import jax
import jax.numpy as jnp

def _softmax(x, axis=-1):
    return jax.nn.softmax(x, axis=axis)

def _gelu(x):
    return jax.nn.gelu(x, approximate=True)

def _silu(x):
    return jax.nn.silu(x)

def _sigmoid(x):
    return jax.nn.sigmoid(x)

def _layernorm(x, axis=-1, eps=1e-05):
    m = jnp.mean(x, axis=axis, keepdims=True)
    v = jnp.var(x, axis=axis, keepdims=True)
    return (x - m) / jnp.sqrt(v + eps)

def _scatter_add(tgt, idx, src, axis=0):
    return tgt.at[idx].add(src)

def _segment_sum(src, seg, n):
    return jax.ops.segment_sum(src, seg, n)
kernel_name = 'mk_gnn_resnorm_d1_gnn_r32_a82b99'

def setup_inputs(seed: int=0):
    np.random.seed(seed)
    _w = jnp.asarray

    def _rec_inputs():
        import jax
        import jax.numpy as jnp
        _gk = jax.random.key(seed)
        x = -0.000202 + 1 * jax.random.normal(jax.random.fold_in(_gk, 1), (3125, 128), jnp.float32)
        src = jax.random.randint(jax.random.fold_in(_gk, 2), (50000,), 0, 3125, jnp.int32)
        dst = jnp.minimum((3125 * jax.random.uniform(jax.random.fold_in(_gk, 3), (50000,)) ** 2.0).astype(jnp.int32), 99999)
        _o = jnp.argsort(dst, stable=True)
        src = src[_o]
        dst = dst[_o]
        edge_type_5 = jax.random.randint(jax.random.fold_in(_gk, 12), (50000,), 0, 5, jnp.int32)
        return (x, src, dst, edge_type_5)
    x, src, dst, edge_type_5 = _rec_inputs()

    def _L0_gnn_setup():
        import jax, jax.numpy as jnp
        import numpy as np
        N = 50000
        E = 20000
        HIDDEN = 128
        R = 5
        HEADS = 8
        HEAD_DIM = HIDDEN // HEADS
        LN_EPS = 1e-05

        def _fused_forward(node_embeddings, W_Q, W_K, W_V, attn_bias, out_proj_w, out_proj_b, ln_gamma, ln_beta, edge_index, edge_types):
            src, dst = (edge_index[0], edge_index[1])
            n = node_embeddings.shape[0]
            x_src = node_embeddings[src]
            x_dst = node_embeddings[dst]
            scale = HEAD_DIM ** 0.5
            NEG = jnp.float32(-1000000000.0)
            out = jnp.zeros((n, HEADS, HEAD_DIM), dtype=node_embeddings.dtype)
            for r in range(R):
                mask = edge_types == r
                q = jnp.einsum('eh,khd->ekd', x_dst, W_Q[r])
                k = jnp.einsum('eh,khd->ekd', x_src, W_K[r])
                v = jnp.einsum('eh,khd->ekd', x_src, W_V[r])
                logits = (q * k).sum(-1) / scale + attn_bias[r][None, :]
                masked_logits = jnp.where(mask[:, None], logits, NEG)
                max_v = jax.ops.segment_max(masked_logits, dst, num_segments=n)
                max_v = jnp.maximum(max_v, NEG)
                exp_l = jnp.where(mask[:, None], jnp.exp(masked_logits - max_v[dst]), 0.0)
                sum_exp = jax.ops.segment_sum(exp_l, dst, num_segments=n)
                attn = exp_l / (sum_exp[dst] + 1e-12)
                out = out + jax.ops.segment_sum(attn[:, :, None] * v, dst, num_segments=n)
            out = out.reshape(n, HIDDEN)
            out = out @ out_proj_w.T + out_proj_b
            h = out + node_embeddings
            mu = h.mean(-1, keepdims=True)
            var = ((h - mu) ** 2).mean(-1, keepdims=True)
            return (h - mu) / jnp.sqrt(var + LN_EPS) * ln_gamma + ln_beta
        key = jax.random.key(seed)
        ks = jax.random.split(key, 10)
        bound = float(np.sqrt(6.0 / (HIDDEN + HEAD_DIM)))
        pbound = float(np.sqrt(1.0 / HIDDEN))
        return {'node_embeddings': jax.random.normal(ks[0], (N, HIDDEN), dtype=jnp.float32), 'edge_index': jax.random.randint(ks[1], (2, E), 0, N, dtype=jnp.int64), 'edge_types': jax.random.randint(ks[2], (E,), 0, R, dtype=jnp.int64), 'W_Q': jax.random.uniform(ks[3], (R, HEADS, HIDDEN, HEAD_DIM), minval=-bound, maxval=bound, dtype=jnp.float32), 'W_K': jax.random.uniform(ks[4], (R, HEADS, HIDDEN, HEAD_DIM), minval=-bound, maxval=bound, dtype=jnp.float32), 'W_V': jax.random.uniform(ks[5], (R, HEADS, HIDDEN, HEAD_DIM), minval=-bound, maxval=bound, dtype=jnp.float32), 'attn_bias': jnp.zeros((R, HEADS), dtype=jnp.float32), 'out_proj_w': jax.random.uniform(ks[6], (HIDDEN, HIDDEN), minval=-pbound, maxval=pbound, dtype=jnp.float32), 'out_proj_b': jax.random.uniform(ks[7], (HIDDEN,), minval=-pbound, maxval=pbound, dtype=jnp.float32), 'ln_gamma': jnp.ones((HIDDEN,), dtype=jnp.float32), 'ln_beta': jnp.zeros((HIDDEN,), dtype=jnp.float32)}
    _L0_gnn_all = _L0_gnn_setup()
    _L0_gnn_in = {k: v for k, v in _L0_gnn_all.items() if k in ('W_Q', 'W_K', 'W_V', 'attn_bias', 'out_proj_w', 'out_proj_b', 'ln_gamma', 'ln_beta')}
    del _L0_gnn_all
    return {'x': x, 'src': src, 'dst': dst, 'edge_type_5': edge_type_5, 'L0_gnn_W_Q': _L0_gnn_in['W_Q'], 'L0_gnn_W_K': _L0_gnn_in['W_K'], 'L0_gnn_W_V': _L0_gnn_in['W_V'], 'L0_gnn_attn_bias': _L0_gnn_in['attn_bias'], 'L0_gnn_out_proj_w': _L0_gnn_in['out_proj_w'], 'L0_gnn_out_proj_b': _L0_gnn_in['out_proj_b'], 'L0_gnn_ln_gamma': _L0_gnn_in['ln_gamma'], 'L0_gnn_ln_beta': _L0_gnn_in['ln_beta']}

def reference(x, src, dst, edge_type_5, L0_gnn_W_Q, L0_gnn_W_K, L0_gnn_W_V, L0_gnn_attn_bias, L0_gnn_out_proj_w, L0_gnn_out_proj_b, L0_gnn_ln_gamma, L0_gnn_ln_beta):
    import jax
    import jax.numpy as jnp

    def _L0_gnn_ref(node_embeddings, edge_index, edge_types, W_Q, W_K, W_V, attn_bias, out_proj_w, out_proj_b, ln_gamma, ln_beta):
        import jax, jax.numpy as jnp
        import numpy as np
        N = 50000
        E = 20000
        HIDDEN = 128
        R = 5
        HEADS = 8
        HEAD_DIM = HIDDEN // HEADS
        LN_EPS = 1e-05

        def _fused_forward(node_embeddings, W_Q, W_K, W_V, attn_bias, out_proj_w, out_proj_b, ln_gamma, ln_beta, edge_index, edge_types):
            src, dst = (edge_index[0], edge_index[1])
            n = node_embeddings.shape[0]
            x_src = node_embeddings[src]
            x_dst = node_embeddings[dst]
            scale = HEAD_DIM ** 0.5
            NEG = jnp.float32(-1000000000.0)
            out = jnp.zeros((n, HEADS, HEAD_DIM), dtype=node_embeddings.dtype)
            for r in range(R):
                mask = edge_types == r
                q = jnp.einsum('eh,khd->ekd', x_dst, W_Q[r])
                k = jnp.einsum('eh,khd->ekd', x_src, W_K[r])
                v = jnp.einsum('eh,khd->ekd', x_src, W_V[r])
                logits = (q * k).sum(-1) / scale + attn_bias[r][None, :]
                masked_logits = jnp.where(mask[:, None], logits, NEG)
                max_v = jax.ops.segment_max(masked_logits, dst, num_segments=n)
                max_v = jnp.maximum(max_v, NEG)
                exp_l = jnp.where(mask[:, None], jnp.exp(masked_logits - max_v[dst]), 0.0)
                sum_exp = jax.ops.segment_sum(exp_l, dst, num_segments=n)
                attn = exp_l / (sum_exp[dst] + 1e-12)
                out = out + jax.ops.segment_sum(attn[:, :, None] * v, dst, num_segments=n)
            out = out.reshape(n, HIDDEN)
            out = out @ out_proj_w.T + out_proj_b
            h = out + node_embeddings
            mu = h.mean(-1, keepdims=True)
            var = ((h - mu) ** 2).mean(-1, keepdims=True)
            return (h - mu) / jnp.sqrt(var + LN_EPS) * ln_gamma + ln_beta
        return _fused_forward(node_embeddings, W_Q, W_K, W_V, attn_bias, out_proj_w, out_proj_b, ln_gamma, ln_beta, edge_index, edge_types)
    edge_index = jnp.stack([src, dst])
    x = _layernorm(x + _L0_gnn_ref(x, edge_index, edge_type_5, L0_gnn_W_Q, L0_gnn_W_K, L0_gnn_W_V, L0_gnn_attn_bias, L0_gnn_out_proj_w, L0_gnn_out_proj_b, L0_gnn_ln_gamma, L0_gnn_ln_beta), axis=-1)
    return x

_drawn_inputs = setup_inputs


def setup_inputs(seed=0):
    import zlib

    import numpy as np

    out = dict(_drawn_inputs(seed))
    spreads = {'L0_gnn_attn_bias': (0.0, 0.8),
     'L0_gnn_ln_gamma': (1.0, 0.2),
     'L0_gnn_ln_beta': (0.0, 0.1)}
    factors = {'L0_gnn_out_proj_b': 3.079}
    for name, (base, spread) in spreads.items():
        noise = np.random.default_rng([zlib.crc32(name.encode()), seed]).standard_normal(out[name].shape)
        drawn = base * np.exp(spread * noise) if base else spread * noise
        out[name] = jnp.asarray(drawn.astype(out[name].dtype))
    for name, factor in factors.items():
        out[name] = (out[name] * factor).astype(out[name].dtype)
    return out
```

```python
from contextlib import ExitStack

import concourse.bass as bass
from concourse import mybir

F32 = mybir.dt.float32
BF16 = mybir.dt.bfloat16
I32 = mybir.dt.int32
ALU = mybir.AluOpType
ACT = mybir.ActivationFunctionType
AX_X = mybir.AxisListType.X

P = 128
BIG = 1.0e30


def gnn_layer(nc, x, src, dst, etype, w_q, w_k, w_v, attn_bias, out_w, out_b, gamma, beta, out):
    N, HID = x.shape
    E = src.shape[0]
    R, H, _, D = w_q.shape
    RH = R * H
    TILES = -(-N // P)
    NPAD = TILES * P
    LASTN = N - (TILES - 1) * P
    ROWS = -(-E // P)
    FULL = E // P
    TAIL = E - FULL * P
    B = 4
    STEPS = -(-(ROWS + TILES - 1) // (2 * B)) * 2 * B
    NB = STEPS // B
    NI = NB // 2
    ROWT = -(-STEPS // P)
    RROWS = ROWS + 1
    KW = HID + H
    PERB = 12
    TBANKS = -(-TILES // PERB)
    SCALE = 1.0 / (D ** 0.5)
    DVE_R = list(range(0, R, 2))
    ACT_R = list(range(1, R, 2))
    CPLUS_DONE = 3
    ROWI_DONE = CPLUS_DONE + 5
    ADDR_DONE = ROWI_DONE + 4 + 2 * (TBANKS - 1)
    DLOC_DONE = ADDR_DONE + 7
    SHIFT_DONE = DLOC_DONE + 3
    assert HID == P and H * D == P and 0 < TAIL < P and B * P == 512 and PERB * RH <= 512

    rec = nc.dram_tensor("edge_rows", [RROWS, 3 * P], I32).ap()
    k_tab = nc.dram_tensor("k_table", [NPAD * R, KW], F32).ap()
    v_tab = nc.dram_tensor("v_table", [NPAD * R, HID], F32).ap()
    q_tab = nc.dram_tensor("q_table", [NPAD * R, HID], F32).ap()
    dflat = nc.dram_tensor("local_dst", [1, ROWT * P * P + 2], F32).ap()

    with ExitStack() as ctx:
        def sb(name, shape, dt=F32):
            return ctx.enter_context(nc.sbuf_tensor(name, shape, dt))

        def sem(name):
            return ctx.enter_context(nc.semaphore(name))

        psum = ctx.enter_context(nc.psum_tensor("psum", [P, 8 * 512], F32))
        bank = [psum[:, 512 * n:512 * (n + 1)] for n in range(8)]
        node_ps = psum[:, 5 * 512:8 * 512]
        agg_ps = psum[:, 0:TILES * HID]

        iota_n = sb("iota_n", [P, P])
        iota_i = sb("iota_i", [P, P], I32)
        ident = sb("ident", [P, P])
        ones = sb("ones", [P, P])
        step_id = sb("step_id", [P, ROWT])
        step_i = sb("step_i", [P, ROWT], I32)
        crow_i = sb("crow_i", [1, RROWS], I32)
        pad_row = sb("pad_row", [1, 3 * P], I32)
        neg5 = sb("neg5", [1, 2])
        x_n = sb("x_n", [P, TILES, HID])
        xs = sb("xs", [P, 2, HID])
        xt = sb("xt", [P, 2, P])
        w_all = sb("w_all", [P, R, 3, HID])
        wo_raw = sb("wo_raw", [P, HID])
        wo_t = sb("wo_t", [P, HID])
        ob_all = sb("ob_all", [P, HID])
        ga_all = sb("ga_all", [P, HID])
        be_all = sb("be_all", [P, HID])
        kst = sb("kst", [P, 2, R, KW])
        vst = sb("vst", [P, 2, R, HID])
        qst = sb("qst", [P, 2, R, HID])
        last_i = sb("last_i", [1, RROWS], I32)
        tile_i = sb("tile_i", [1, RROWS], I32)
        crow = sb("crow", [1, RROWS])
        cplus = sb("cplus", [1, RROWS])
        row_f = sb("row_f", [P, ROWT])
        row_i = sb("row_i", [P, ROWT], I32)
        tile_f = sb("tile_f", [P, ROWT])
        ge1 = sb("ge1", [P, ROWT])
        ge2 = sb("ge2", [P, ROWT])
        addr2 = sb("addr2", [P, ROWT, 2])
        addr_row = sb("addr_row", [1, 2, ROWT * P], I32)
        erow = sb("erow", [P, ROWT, 3, P], I32)
        kidx = sb("kidx", [P, ROWT * P])
        qidx = sb("qidx", [P, ROWT * P])
        ety = sb("ety", [P, ROWT * P])
        dloc = sb("dloc", [P, ROWT * P])
        pen = sb("pen", [P, ROWT * P])
        islast = sb("islast", [P, ROWT * P])
        tmask = sb("tmask", [P, STEPS, R])
        tpen = sb("tpen", [P, STEPS, R])
        logit = sb("logit", [P, STEPS, H])
        prob = sb("prob", [P, STEPS, H])
        attn = sb("attn", [P, STEPS, H])
        flat_l, flat_p, flat_a = (t[:].rearrange("p s h -> p (s h)") for t in (logit, prob, attn))
        erf = flat_p[:, 0:6 * ROWT * P].rearrange("p (n k e) -> p n k e", n=6, k=ROWT)
        esf = flat_a[:, 0:3 * ROWT * P].rearrange("p (k n e) -> p k n e", k=ROWT, n=3)
        less = flat_a[:, 3 * ROWT * P:3 * ROWT * P + ROWT * RROWS].rearrange("p (k c) -> p k c", k=ROWT)
        shl = flat_l[:, 0:2 * ROWT * P].rearrange("p (n k e) -> p n k e", n=2, k=ROWT)
        ist = sb("ist", [P, 2, 2, B], I32)
        pst = sb("pst", [P, 2, B])
        kg = sb("kg", [P, 2, B, KW])
        qg = sb("qg", [P, 2, B, HID])
        prod = sb("prod", [P, 2, B, HID])
        lsum = sb("lsum", [P, 2, B, H])
        ml = sb("ml", [P, 2, B, R, H])
        oh = sb("oh", [P, 4, B, P])
        oht = sb("oht", [P, 2, B, P])
        pen_s = sb("pen_s", [RH, 2, B * P])
        fwd = sb("fwd", [RH, 2, B * P])
        fe = sb("fe", [P, 2, B, RH])
        sel = sb("sel", [P, 2, B, R, H])
        tsel = sb("tsel", [P, 2, B, H])
        zed = sb("zed", [P, 2, B, H])
        pm = sb("pm", [P, 2, B, R, H])
        node_max = sb("node_max", [P, TBANKS * 512])
        node_den = sb("node_den", [P, TBANKS * 512])
        agg = logit[:].rearrange("p s h -> p (s h)")[:, 0:TILES * HID].rearrange("p (t c) -> p t c", t=TILES)
        hh = prob[:].rearrange("p s h -> p (s h)")[:, 0:TILES * HID].rearrange("p (t c) -> p t c", t=TILES)
        sq = attn[:].rearrange("p s h -> p (s h)")[:, 0:TILES * HID].rearrange("p (t c) -> p t c", t=TILES)
        agt = sb("agt", [P, 2, P])
        mu = sb("mu", [P, TILES])
        var = sb("var", [P, TILES])

        s = {n: sem(n) for n in (
            "s_x s_xs0 s_xs1 s_w s_wo s_vecs s_bias s_pad s_ip s_rec s_lastd s_const s_id s_wot "
            "sch sch_ps s_erow s_dfl s_shl addr_ps addr_rdy tr_ps tr_sb edges_rdy zero_rdy "
            "xt_ps xt_sb tab_mm tab_dve tab_act tab_out0 tab_out1 "
            "ist_ready pst_ready kq0 kq1 logit_done ml_ready oh_ready mlt_ready pens_ready f_ready fb_ready fe_ready tmax_mm "
            "nmax_rdy zero1 dve_b dve_c dve_d dve_v dve_t "
            "c_oh c_ohtp c_oht c_ex c_sel c_z c_p c_pm c_den "
            "nden_rdy zero2 d_oh d_ohtp d_oht d_ex d_sel "
            "vist_ready v0 v1 wv_ready v_mm agg_rdy "
            "o_tr o_cp o_mm o_ev fin s_out sq_ask sq_got pool_turn act_turn sp_turn pe_turn dve_turn").split()}

        CREDIT = 4

        def upto(b):
            return b + CREDIT + 1

        x_full = x[0:(TILES - 1) * P, :].rearrange("(t p) d -> p t d", p=P)
        out_full = out[0:(TILES - 1) * P, :].rearrange("(t p) d -> p t d", p=P)

        block = ctx.enter_context(nc.Block())

        def addr_of(pe, which, step):
            return pe.value_load(addr_row[0:1, which, bass.ds(step, 1)], min_val=0,
                                 max_val=(TILES - 1) * P if which else (TBANKS - 1) * 512 + PERB * RH)

        @block.sync
        def _(sp):
            sp.wait_ge(s["s_pad"], 2)
            for n, a in enumerate((src, dst, etype)):
                sp.dma_start(rec[0:FULL, n * P:(n + 1) * P], a[0:FULL * P].rearrange("(c e) -> c e", e=P)).then_inc(s["s_rec"], 16)
                sp.dma_start(rec[FULL:FULL + 1, n * P:n * P + TAIL], a[FULL * P:E].rearrange("(c e) -> c e", c=1)).then_inc(s["s_rec"], 16)
                sp.dma_start(rec[FULL:FULL + 1, n * P + TAIL:(n + 1) * P], pad_row[:, n * P + TAIL:(n + 1) * P]).then_inc(s["s_rec"], 16)
            sp.dma_start(rec[ROWS:RROWS, :], pad_row[:, :]).then_inc(s["s_rec"], 16)
            sp.wait_ge(s["s_rec"], 160)
            sp.dma_start(last_i[:], rec.rearrange("c e -> e c")[2 * P - 1:2 * P, :], allow_slow_non_contiguous=True).then_inc(s["s_lastd"], 16)
            sp.wait_ge(s["sch"], DLOC_DONE)
            sp.dma_start(dflat[:, 1:ROWT * P * P + 1].rearrange("o (k p e) -> (o p) k e", k=ROWT, e=P), erf[:, 3, :, :]).then_inc(s["s_dfl"], 16)
            sp.dma_start(dflat[:, 0:1], neg5[:, 0:1]).then_inc(s["s_dfl"], 16)
            sp.dma_start(dflat[:, ROWT * P * P + 1:ROWT * P * P + 2], neg5[:, 1:2]).then_inc(s["s_dfl"], 16)
            sp.wait_ge(s["s_dfl"], 48)
            sp.dma_start(shl[:, 0, :, :], dflat[:, 0:ROWT * P * P].rearrange("o (k p e) -> (o p) k e", k=ROWT, e=P)).then_inc(s["s_shl"], 16)
            sp.dma_start(shl[:, 1, :, :], dflat[:, 2:ROWT * P * P + 2].rearrange("o (k p e) -> (o p) k e", k=ROWT, e=P)).then_inc(s["s_shl"], 16)

            def load_tile(t, j):
                sp.dma_start(xs[:, j, :], x[bass.ds(t * P, P), :]).then_inc(s["s_xs0"] if j == 0 else s["s_xs1"], 16)

            def store_tile(t, j):
                done = s["tab_out0"] if j == 0 else s["tab_out1"]
                sp.wait_ge(s["tab_dve"], len(DVE_R) * (t + 1))
                sp.sem_inc(s["sp_turn"], 1)
                sp.wait_ge(s["tab_act"], len(ACT_R) * (t + 1))
                sp.sem_inc(s["sp_turn"], 1)
                sp.dma_start(k_tab[bass.ds(t * (P * R), P * R), :].rearrange("(p r) c -> p r c", r=R), kst[:, j, :, :]).then_inc(done, 16)
                sp.dma_start(v_tab[bass.ds(t * (P * R), P * R), :].rearrange("(p r) c -> p r c", r=R), vst[:, j, :, :]).then_inc(done, 16)
                sp.dma_start(q_tab[bass.ds(t * (P * R), P * R), :].rearrange("(p r) c -> p r c", r=R), qst[:, j, :, :]).then_inc(done, 16)

            load_tile(0, 0)
            load_tile(1, 1)
            with sp.Fori(0, TILES // 2 - 1) as i:
                for j in range(2):
                    sp.wait_ge(s["xt_ps"], 2 * i + j + 1)
                    sp.sem_inc(s["sp_turn"], 1)
                    load_tile(2 * i + j + 2, j)
                    store_tile(2 * i + j, j)
            sp.wait_ge(s["xt_ps"], TILES - 2)
            sp.dma_start(xs[0:LASTN, 0, :], x[(TILES - 1) * P:N, :]).then_inc(s["s_xs0"], 16)
            for t in range(TILES - 3, TILES):
                store_tile(t, t % 2)
            sp.dma_start(x_n[:, 0:TILES - 1, :], x_full).then_inc(s["s_x"], 16)
            sp.dma_start(x_n[0:LASTN, TILES - 1, :], x[(TILES - 1) * P:N, :]).then_inc(s["s_x"], 16)

            sp.wait_ge(s["fin"], 1)
            sp.dma_start(out_full, sq[:, 0:TILES - 1, :]).then_inc(s["s_out"], 16)
            sp.dma_start(out[(TILES - 1) * P:N, :], sq[0:LASTN, TILES - 1, :]).then_inc(s["s_out"], 16)
            sp.wait_ge(s["s_out"], 32)

        @block.gpsimd
        def _(pool):
            nc.gpsimd.memset(pad_row[:, 0:3 * P], 0).then_inc(s["s_ip"], 1)
            pool.wait_ge(s["s_ip"], 1)
            nc.gpsimd.memset(pad_row[:, P:2 * P], NPAD - 1).then_inc(s["s_pad"], 1)
            nc.gpsimd.memset(neg5[:], -5.0e5).then_inc(s["s_pad"], 1)
            nc.gpsimd.iota(iota_i[:], [[1, P]], base=0, channel_multiplier=0).then_inc(s["s_const"], 1)
            nc.gpsimd.iota(crow_i[:], [[1, RROWS]], base=0, channel_multiplier=0).then_inc(s["s_const"], 1)
            nc.gpsimd.iota(step_i[:], [[P, ROWT]], base=0, channel_multiplier=1).then_inc(s["s_const"], 1)
            nc.gpsimd.memset(ones[:], 1.0).then_inc(s["s_const"], 1)
            nc.gpsimd.memset(ident[:], 0.0).then_inc(s["s_id"], 1)
            pool.wait_ge(s["s_id"], 1)
            nc.gpsimd.affine_select(out=ident[:], in_=ident[:], compare_op=ALU.not_equal, fill=1.0, base=0,
                                    pattern=[[-1, P]], channel_multiplier=1).then_inc(s["s_id"], 1)
            pool.wait_ge(s["s_rec"], 160)
            pool.wait_ge(s["sch"], ROWI_DONE)
            for k in range(ROWT):
                nc.gpsimd.indirect_dma_start(erow[:, k, :, :].rearrange("p a e -> p (a e)"), None, rec,
                                             bass.IndirectOffsetOnAxis(ap=row_i[:, k:k + 1], axis=0)).then_inc(s["s_erow"], 16)
            pool.wait_ge(s["tab_out0"], 48 * (TILES - TILES // 2))
            pool.wait_ge(s["tab_out1"], 48 * (TILES // 2))
            with pool.Fori(0, NI) as i:
                for j in range(2):
                    b = 2 * i + j
                    pool.wait_ge(s["ist_ready"], upto(b))
                    pool.sem_inc(s["pool_turn"], 1)
                    done = s["kq0"] if j == 0 else s["kq1"]
                    for k in range(B):
                        nc.gpsimd.indirect_dma_start(kg[:, j, k, :], None, k_tab, bass.IndirectOffsetOnAxis(ap=ist[:, j, 0, k:k + 1], axis=0)).then_inc(done, 16)
                        nc.gpsimd.indirect_dma_start(qg[:, j, k, :], None, q_tab, bass.IndirectOffsetOnAxis(ap=ist[:, j, 1, k:k + 1], axis=0)).then_inc(done, 16)
            with pool.Fori(0, NI) as i:
                for j in range(2):
                    b = 2 * i + j
                    pool.wait_ge(s["vist_ready"], upto(b))
                    pool.sem_inc(s["pool_turn"], 1)
                    done = s["v0"] if j == 0 else s["v1"]
                    for k in range(B):
                        nc.gpsimd.indirect_dma_start(qg[:, j, k, :], None, v_tab, bass.IndirectOffsetOnAxis(ap=ist[:, j, 0, k:k + 1], axis=0)).then_inc(done, 16)

        @block.scalar
        def _(act):
            for name in ("ist_ready", "pst_ready", "pens_ready", "fe_ready", "c_oht", "c_p", "d_oht", "vist_ready"):
                act.sem_inc(s[name], CREDIT)
            for j in range(2):
                for r in range(R):
                    act.dma_start(kst[:, j, r, HID:KW], attn_bias[r:r + 1, :].broadcast_to((P, H))).then_inc(s["s_bias"], 16)
            for n, w in ((0, w_k), (1, w_v), (2, w_q)):
                for r in range(R):
                    act.dma_start(w_all[:, r, n, :].rearrange("k (h d) -> k h d", h=H), w[r].rearrange("h k d -> k h d")).then_inc(s["s_w"], 16)
            act.dma_start(wo_raw[:], out_w).then_inc(s["s_wo"], 16)
            for t, v in ((ob_all, out_b), (ga_all, gamma), (be_all, beta)):
                act.dma_start(t[:], v.rearrange("(a c) -> a c", a=1).broadcast_to((P, HID))).then_inc(s["s_vecs"], 16)

            def table_tile(t, j, free):
                act.wait_ge(s["xt_ps"], t + 1)
                nc.scalar.copy(xt[:, j, :], bank[5 + j][:, 0:P]).then_inc(s["xt_sb"], 1)
                if free is not None:
                    act.wait_ge(*free)
                for r in ACT_R:
                    act.wait_ge(s["tab_mm"], R * t + r + 1)
                    nc.scalar.copy(kst[:, j, r, 0:HID], bank[r][:, 0:HID])
                    nc.scalar.copy(vst[:, j, r, :], bank[r][:, HID:2 * HID])
                    nc.scalar.mul(qst[:, j, r, :], bank[r][:, 2 * HID:3 * HID], SCALE).then_inc(s["tab_act"], 1)

            for t in range(2):
                table_tile(t, t, None)
            with act.Fori(1, TILES // 2) as i:
                for j in range(2):
                    table_tile(2 * i + j, j, (s["tab_out0"] if j == 0 else s["tab_out1"], 48 * i))
            table_tile(TILES - 1, 0, (s["tab_out0"], 48 * (TILES // 2)))

            act.wait_ge(s["edges_rdy"], 1)
            with act.Fori(0, NI) as i:
                for j in range(2):
                    b = 2 * i + j
                    act.wait_ge(s["logit_done"], upto(b - 2))
                    act.sem_inc(s["act_turn"], 1)
                    nc.scalar.copy(ist[:, j, 0, :], kidx[:, bass.ds(B * b, B)])
                    nc.scalar.copy(ist[:, j, 1, :], qidx[:, bass.ds(B * b, B)]).then_inc(s["ist_ready"], 1)
                    act.wait_ge(s["mlt_ready"], upto(b - 2))
                    act.sem_inc(s["act_turn"], 1)
                    nc.scalar.copy(pst[:, j, :], pen[:, bass.ds(B * b, B)]).then_inc(s["pst_ready"], 1)
                    act.wait_ge(s["mlt_ready"], upto(b))
                    nc.scalar.copy(pen_s[:, j, :], bank[2 + j][0:RH, :]).then_inc(s["pens_ready"], 1)
                    act.wait_ge(s["tmax_mm"], upto(b - 2))
                    act.wait_ge(s["fb_ready"], upto(b))
                    act.sem_inc(s["act_turn"], 1)
                    for k in range(B):
                        last = nc.scalar.activation(fe[:, j, k, :], bank[4][:, (j * B + k) * RH:(j * B + k + 1) * RH], ACT.Copy,
                                                    scale=islast[:, bass.ds(B * b + k, 1)])
                    last.then_inc(s["fe_ready"], 1)

            def one_hot_back(b, j, ready, done, used):
                act.wait_ge(used, upto(b - 2))
                act.wait_ge(ready, upto(b))
                nc.scalar.copy(oht[:, j, :, :].rearrange("p b n -> p (b n)"), bank[j]).then_inc(done, 1)

            with act.Fori(0, NI) as i:
                for j in range(2):
                    b = 2 * i + j
                    one_hot_back(b, j, s["c_ohtp"], s["c_oht"], s["c_ex"])
                    act.wait_ge(s["c_z"], upto(b))
                    act.sem_inc(s["act_turn"], 1)
                    nc.scalar.activation(prob[:, bass.ds(B * b, B), :], zed[:, j, :, :], ACT.Exp).then_inc(s["c_p"], 1)
            with act.Fori(0, NI) as i:
                for j in range(2):
                    one_hot_back(2 * i + j, j, s["d_ohtp"], s["d_oht"], s["d_ex"])
            with act.Fori(0, NI) as i:
                for j in range(2):
                    b = 2 * i + j
                    act.wait_ge(s["wv_ready"], upto(b - 2))
                    act.wait_ge(s["v_mm"], upto(b - 2))
                    act.sem_inc(s["act_turn"], 1)
                    nc.scalar.copy(ist[:, j, 0, :], kidx[:, bass.ds(B * b, B)]).then_inc(s["vist_ready"], 1)
            for t in range(TILES):
                act.wait_ge(s["o_tr"], t + 1)
                if t >= 2:
                    act.wait_ge(s["o_mm"], t - 1)
                nc.scalar.copy(agt[:, t % 2, :], bank[t % 2][:, 0:P]).then_inc(s["o_cp"], 1)
            for n in range(2):
                act.wait_ge(s["sq_ask"], n + 1)
                nc.scalar.activation(var[:], var[:], ACT.Sqrt).then_inc(s["sq_got"], 1)

        @block.tensor
        def _(pe):
            mm = nc.tensor.matmul
            for name in ("mlt_ready", "fb_ready", "tmax_mm", "c_ohtp", "c_ex", "c_den", "d_ohtp", "d_ex", "v_mm"):
                pe.sem_inc(s[name], CREDIT)

            def addr_of(which, step):
                return pe.value_load(addr_row[0:1, which, bass.ds(step, 1)], min_val=0,
                                     max_val=(TILES - 1) * P if which else TBANKS * 512 - RH)

            pe.wait_ge(s["s_id"], 2)
            pe.wait_ge(s["s_wo"], 16)
            nc.tensor.transpose(bank[7][:, 0:P], wo_raw[:], ident[:]).then_inc(s["s_wot"], 1)
            pe.wait_ge(s["s_const"], 4)
            pe.wait_ge(s["sch"], CPLUS_DONE)
            mm(bank[0][:, 0:RROWS], ones[0:1, :], cplus[:], start=True, stop=True).then_inc(s["sch_ps"], 1)
            pe.wait_ge(s["sch"], ADDR_DONE)
            for n in range(2):
                for k in range(ROWT):
                    last = mm(bank[1 + n][0:1, k * P:(k + 1) * P], addr2[:, k, n:n + 1], ident[:], start=True, stop=True)
            last.then_inc(s["addr_ps"], 1)
            for n in range(6):
                if n == 0:
                    pe.wait_ge(s["sch"], DLOC_DONE)
                if n == 4:
                    pe.wait_ge(s["sch"], SHIFT_DONE)
                if n >= 2:
                    pe.wait_ge(s["tr_sb"], n - 1)
                for k in range(ROWT):
                    last = nc.tensor.transpose(bank[3 + n % 2][:, k * P:(k + 1) * P], erf[:, n, k, :], ident[:])
                last.then_inc(s["tr_ps"], 1)

            pe.wait_ge(s["s_w"], 48 * R)
            pe.wait_ge(s["edges_rdy"], 1)

            def table_tile(t, j, loads, first):
                pe.wait_ge(s["s_xs0"] if j == 0 else s["s_xs1"], loads)
                if not first:
                    pe.wait_ge(s["xt_sb"], t)
                nc.tensor.transpose(bank[5 + j][:, 0:P], xs[:, j, :], ident[:]).then_inc(s["xt_ps"], 1)
                pe.wait_ge(s["xt_sb"], t + 1)
                for r in range(R):
                    if not first:
                        if r in DVE_R:
                            pe.wait_ge(s["tab_dve"], len(DVE_R) * t - len(DVE_R) + DVE_R.index(r) + 1)
                        else:
                            pe.wait_ge(s["tab_act"], len(ACT_R) * t - len(ACT_R) + ACT_R.index(r) + 1)
                    mm(bank[r][:, 0:3 * HID], xt[:, j, :], w_all[:, r, :, :].rearrange("k a c -> k (a c)"),
                       start=True, stop=True).then_inc(s["tab_mm"], 1)

            for t in range(2):
                table_tile(t, t, 16, t == 0)
            with pe.Fori(1, TILES // 2) as i:
                for j in range(2):
                    table_tile(2 * i + j, j, 16 * i + 16, False)
            table_tile(TILES - 1, 0, 16 * (TILES // 2 + 1), False)

            pe.wait_ge(s["zero_rdy"], 1)
            with pe.Fori(0, NI) as i:
                for j in range(2):
                    b = 2 * i + j
                    pe.wait_ge(s["pst_ready"], upto(b))
                    pe.wait_ge(s["f_ready"], upto(b - 2))
                    pe.wait_ge(s["ml_ready"], upto(b))
                    pe.sem_inc(s["pe_turn"], 1)
                    for k in range(B):
                        nc.tensor.transpose(bank[j][0:RH, k * P:(k + 1) * P], ml[:, j, k, :, :].rearrange("p r h -> p (r h)"), ident[:])
                    for k in range(B):
                        last = nc.tensor.transpose(bank[2 + j][0:RH, k * P:(k + 1) * P], pst[:, j, k:k + 1].broadcast_to((P, RH)), ident[:])
                    last.then_inc(s["mlt_ready"], 1)
                    pe.wait_ge(s["fe_ready"], upto(b - 2))
                    pe.wait_ge(s["f_ready"], upto(b))
                    pe.sem_inc(s["pe_turn"], 1)
                    for k in range(B):
                        last = nc.tensor.transpose(bank[4][:, (j * B + k) * RH:(j * B + k + 1) * RH], fwd[:, j, k * P:(k + 1) * P], ident[0:RH, 0:RH])
                    last.then_inc(s["fb_ready"], 1)
                    pe.wait_ge(s["oh_ready"], upto(b))
                    pe.wait_ge(s["fe_ready"], upto(b))
                    pe.sem_inc(s["pe_turn"], 1)
                    for k in range(B):
                        last = mm(node_ps[:, bass.ds(addr_of(0, B * b + k), RH)], oh[:, j, k, :], fe[:, j, k, :],
                                  start=False, stop=True, skip_group_check=True)
                    last.then_inc(s["tmax_mm"], 1)

            def turn_and_expand(b, j, j4, made, turned, back, expanded, taken, table):
                pe.wait_ge(back, upto(b - 2))
                pe.wait_ge(made, upto(b))
                for k in range(B):
                    last = nc.tensor.transpose(bank[j][:, k * P:(k + 1) * P], oh[:, j4, k, :], ident[:])
                last.then_inc(turned, 1)
                pe.wait_ge(taken, upto(b - 2))
                pe.wait_ge(back, upto(b))
                pe.sem_inc(s["pe_turn"], 1)
                for k in range(B):
                    last = mm(bank[2 + j][:, k * RH:(k + 1) * RH], oht[:, j, k, :], table[:, bass.ds(addr_of(0, B * b + k), RH)],
                              start=True, stop=True)
                last.then_inc(expanded, 1)

            pe.wait_ge(s["nmax_rdy"], 1)
            with pe.Fori(0, NB // 4) as i:
                for j4 in range(4):
                    b = 4 * i + j4
                    turn_and_expand(b, j4 % 2, j4, s["c_oh"], s["c_ohtp"], s["c_oht"], s["c_ex"], s["c_sel"], node_max)
                    pe.wait_ge(s["c_pm"], upto(b))
                    pe.sem_inc(s["pe_turn"], 1)
                    for k in range(B):
                        last = mm(node_ps[:, bass.ds(addr_of(0, B * b + k), RH)], oh[:, j4, k, :],
                                  pm[:, j4 % 2, k, :, :].rearrange("p r h -> p (r h)"), start=False, stop=True, skip_group_check=True)
                    last.then_inc(s["c_den"], 1)
            pe.wait_ge(s["nden_rdy"], 1)
            with pe.Fori(0, NB // 4) as i:
                for j4 in range(4):
                    turn_and_expand(4 * i + j4, j4 % 2, j4, s["d_oh"], s["d_ohtp"], s["d_oht"], s["d_ex"], s["d_sel"], node_den)
            pe.wait_ge(s["zero2"], 1)
            with pe.Fori(0, NI) as i:
                for j in range(2):
                    b = 2 * i + j
                    pe.wait_ge(s["wv_ready"], upto(b))
                    pe.sem_inc(s["pe_turn"], 1)
                    for k in range(B):
                        last = mm(agg_ps[:, bass.ds(addr_of(1, B * b + k), HID)], oh[:, j, k, :], prod[:, j, k, :],
                                  start=False, stop=True, skip_group_check=True)
                    last.then_inc(s["v_mm"], 1)

            def project(t):
                pe.wait_ge(s["o_cp"], t + 1)
                if t >= 2:
                    pe.wait_ge(s["o_ev"], t - 1)
                mm(bank[2 + t % 2][:, 0:HID], agt[:, t % 2, :], wo_t[:], start=True, stop=True).then_inc(s["o_mm"], 1)

            pe.wait_ge(s["agg_rdy"], 1)
            for t in range(TILES):
                if t >= 2:
                    pe.wait_ge(s["o_cp"], t - 1)
                nc.tensor.transpose(bank[t % 2][:, 0:P], agg[:, t, :], ident[:]).then_inc(s["o_tr"], 1)
                if t >= 1:
                    project(t - 1)
            project(TILES - 1)

        @block.vector
        def _(dve):
            V = nc.vector
            for name in ("logit_done", "ml_ready", "oh_ready", "f_ready", "c_oh", "c_sel", "c_z", "c_pm", "d_oh", "d_sel", "wv_ready"):
                dve.sem_inc(s[name], CREDIT)

            class Chain:

                def __init__(self, name, base=0):
                    self.sem, self.n, self.base = s[name], 0, base

                def link(self, ins):
                    self.n += 1
                    ins.then_inc(self.sem, 1)
                    dve.wait_ge(self.sem, self.base + self.n)

            sch = Chain("sch")
            dve.wait_ge(s["s_const"], 4)
            dve.wait_ge(s["s_lastd"], 16)
            sch.link(V.tensor_scalar(tile_i[:], last_i[:], 7, None, ALU.logical_shift_right))
            sch.link(V.tensor_copy(crow[:], crow_i[:]))
            sch.link(V.tensor_tensor(cplus[:], tile_i[:], crow[:], ALU.add))
            assert sch.n == CPLUS_DONE
            sch.link(V.tensor_copy(step_id[:], step_i[:]))
            sch.link(V.tensor_copy(iota_n[:], iota_i[:]))
            dve.wait_ge(s["sch_ps"], 1)
            for k in range(ROWT):
                V.tensor_scalar(less[:, k, :], bank[0][:, 0:RROWS], step_id[:, k:k + 1], None, ALU.is_lt).then_inc(s["dve_turn"], 1)
            dve.wait_ge(s["dve_turn"], ROWT)
            sch.link(V.tensor_reduce(row_f[:], less[:], AX_X, ALU.add))
            sch.link(V.tensor_scalar(row_f[:], row_f[:], float(ROWS), None, ALU.min))
            sch.link(V.tensor_copy(row_i[:], row_f[:]))
            assert sch.n == ROWI_DONE
            sch.link(V.tensor_tensor(tile_f[:], step_id[:], row_f[:], ALU.subtract))
            sch.link(V.tensor_scalar(tile_f[:], tile_f[:], float(TILES - 1), None, ALU.min))
            sch.link(V.tensor_scalar(addr2[:, :, 0], tile_f[:], float(RH), None, ALU.mult))
            for m in range(1, TBANKS):
                sch.link(V.tensor_scalar(ge1[:], tile_f[:], float(PERB * m), float(512 - PERB * RH), ALU.is_ge, ALU.mult))
                sch.link(V.tensor_tensor(addr2[:, :, 0], addr2[:, :, 0], ge1[:], ALU.add))
            sch.link(V.tensor_scalar(addr2[:, :, 1], tile_f[:], float(P), None, ALU.mult))
            assert sch.n == ADDR_DONE
            dve.wait_ge(s["addr_ps"], 1)
            V.tensor_copy(addr_row[:, 0, :], bank[1][0:1, :]).then_inc(s["addr_rdy"], 1)
            V.tensor_copy(addr_row[:, 1, :], bank[2][0:1, :]).then_inc(s["addr_rdy"], 1)
            dve.wait_ge(s["s_erow"], 16 * ROWT)
            sch.link(V.tensor_copy(esf[:], erow[:]))
            sch.link(V.tensor_scalar(erf[:, 0, :, :], esf[:, :, 0, :], float(R), None, ALU.mult))
            sch.link(V.tensor_tensor(erf[:, 0, :, :], erf[:, 0, :, :], esf[:, :, 2, :], ALU.add))
            sch.link(V.tensor_scalar(erf[:, 1, :, :], esf[:, :, 1, :], float(R), None, ALU.mult))
            sch.link(V.tensor_tensor(erf[:, 1, :, :], erf[:, 1, :, :], esf[:, :, 2, :], ALU.add))
            sch.link(V.tensor_copy(erf[:, 2, :, :], esf[:, :, 2, :]))
            sch.link(V.tensor_tensor(erf[:, 3, :, :], esf[:, :, 1, :], addr2[:, :, 1:2].broadcast_to((P, ROWT, P)), ALU.subtract))
            assert sch.n == DLOC_DONE
            dve.wait_ge(s["s_shl"], 32)
            sch.link(V.tensor_tensor(erf[:, 4, :, :], erf[:, 3, :, :], shl[:, 0, :, :], ALU.not_equal))
            sch.link(V.tensor_scalar(erf[:, 4, :, :], erf[:, 4, :, :], -BIG, None, ALU.mult))
            sch.link(V.tensor_tensor(erf[:, 5, :, :], erf[:, 3, :, :], shl[:, 1, :, :], ALU.not_equal))
            assert sch.n == SHIFT_DONE
            for n, t in enumerate((kidx, qidx, ety, dloc, pen, islast)):
                dve.wait_ge(s["tr_ps"], n + 1)
                V.tensor_copy(t[:], bank[3 + n % 2]).then_inc(s["tr_sb"], 1)
            dve.wait_ge(s["tr_sb"], 6)
            for r in range(R):
                V.tensor_scalar(tmask[:, :, r], ety[:, 0:STEPS], float(r), None, ALU.is_equal).then_inc(s["dve_turn"], 1)
            dve.wait_ge(s["dve_turn"], ROWT + R)
            V.tensor_scalar(tpen[:], tmask[:], 1.0, BIG, ALU.subtract, ALU.mult).then_inc(s["edges_rdy"], 1)
            dve.wait_ge(s["s_wot"], 1)
            V.tensor_copy(wo_t[:], bank[7][:, 0:P]).then_inc(s["dve_turn"], 1)
            V.memset(fwd[:, 1, B * P - 1:B * P], -BIG).then_inc(s["dve_turn"], 1)
            V.memset(x_n[:, TILES - 1, :], 0.0).then_inc(s["dve_turn"], 1)

            dve.wait_ge(s["s_bias"], 32 * R)

            def table_tile(t, j, free):
                if free is not None:
                    dve.wait_ge(*free)
                for r in DVE_R:
                    dve.wait_ge(s["tab_mm"], R * t + r + 1)
                    V.tensor_copy(kst[:, j, r, 0:HID], bank[r][:, 0:HID])
                    V.tensor_copy(vst[:, j, r, :], bank[r][:, HID:2 * HID])
                    V.tensor_scalar(qst[:, j, r, :], bank[r][:, 2 * HID:3 * HID], SCALE, None, ALU.mult).then_inc(s["tab_dve"], 1)

            for t in range(2):
                table_tile(t, t, None)
            with dve.Fori(1, TILES // 2) as i:
                for j in range(2):
                    table_tile(2 * i + j, j, (s["tab_out0"] if j == 0 else s["tab_out1"], 48 * i))
            table_tile(TILES - 1, 0, (s["tab_out0"], 48 * (TILES // 2)))
            V.memset(node_ps, 0.0).then_inc(s["zero_rdy"], 1)

            def one_hots(b, slot, done):
                for k in range(B):
                    last = V.tensor_scalar(oh[:, slot, k, :], iota_n[:], dloc[:, bass.ds(B * b + k, 1)], None, ALU.is_equal)
                last.then_inc(done, 1)

            def per_type(t, b):
                return t[:, bass.ds(B * b, B), :].unsqueeze(3).broadcast_to((P, B, R, H))

            PER_B = 3
            with dve.Fori(0, NI) as i:
                for j in range(2):
                    b = 2 * i + j
                    c = Chain("dve_b", PER_B * b)
                    dve.wait_ge(s["kq0"] if j == 0 else s["kq1"], 32 * B * i + 32 * B)
                    c.link(V.tensor_tensor(prod[:, j, :, :], kg[:, j, :, 0:HID], qg[:, j, :, :], ALU.mult))
                    c.link(V.tensor_reduce(lsum[:, j, :, :], prod[:, j, :, :].rearrange("p b (h d) -> p b h d", h=H), AX_X, ALU.add))
                    V.tensor_tensor(logit[:, bass.ds(B * b, B), :], lsum[:, j, :, :], kg[:, j, :, HID:KW], ALU.add).then_inc(s["logit_done"], 1)
                    dve.wait_ge(s["tmax_mm"], upto(b - 2))
                    dve.wait_ge(s["logit_done"], upto(b))
                    c.link(V.tensor_tensor(ml[:, j, :, :, :], logit[:, bass.ds(B * b, B), :].unsqueeze(2).broadcast_to((P, B, R, H)),
                                           per_type(tmask, b), ALU.mult))
                    V.tensor_tensor(ml[:, j, :, :, :], ml[:, j, :, :, :], per_type(tpen, b), ALU.add).then_inc(s["ml_ready"], 1)
                    one_hots(b, j, s["oh_ready"])
                    dve.wait_ge(s["f_ready"], upto(b - 1))
                    dve.wait_ge(s["mlt_ready"], upto(b))
                    dve.wait_ge(s["pens_ready"], upto(b))
                    V.tensor_tensor_scan(fwd[:, j, :], pen_s[:, j, :], bank[j][0:RH, :], fwd[:, 1 - j, B * P - 1:B * P],
                                         ALU.add, ALU.max).then_inc(s["f_ready"], 1)
                    assert c.n == PER_B
            dve.wait_ge(s["tmax_mm"], upto(NB - 1))
            V.tensor_copy(node_max[:], node_ps).then_inc(s["dve_turn"], 1)
            dve.wait_ge(s["dve_turn"], ROWT + R + 4)
            V.memset(node_ps, 0.0).then_inc(s["nmax_rdy"], 1)

            PER_C = 3

            def softmax_batch(b, j, slot, ahead):
                c = Chain("dve_c", PER_C * b)
                dve.wait_ge(s["c_ex"], upto(b))
                c.link(V.tensor_tensor(sel[:, j, :, :, :], bank[2 + j][:, 0:B * RH].rearrange("p (b r h) -> p b r h", b=B, r=R),
                                       per_type(tmask, b), ALU.mult))
                dve.sem_inc(s["c_sel"], 1)
                c.link(V.tensor_reduce(tsel[:, j, :, :], sel[:, j, :, :, :].rearrange("p b r h -> p b h r"), AX_X, ALU.add))
                c.link(V.tensor_tensor(zed[:, j, :, :], logit[:, bass.ds(B * b, B), :], tsel[:, j, :, :], ALU.subtract))
                V.tensor_scalar(zed[:, j, :, :], zed[:, j, :, :], 0.0, None, ALU.min).then_inc(s["c_z"], 1)
                if ahead:
                    dve.wait_ge(s["c_den"], upto(b - 2))
                    one_hots(b + 2, (slot + 2) % 4, s["c_oh"])
                dve.wait_ge(s["c_p"], upto(b))
                V.tensor_tensor(pm[:, j, :, :, :], prob[:, bass.ds(B * b, B), :].unsqueeze(2).broadcast_to((P, B, R, H)),
                                per_type(tmask, b), ALU.mult).then_inc(s["c_pm"], 1)
                assert c.n == PER_C

            one_hots(0, 0, s["c_oh"])
            one_hots(1, 1, s["c_oh"])
            with dve.Fori(0, NB // 4 - 1) as i:
                for j4 in range(4):
                    softmax_batch(4 * i + j4, j4 % 2, j4, True)
            for j4 in range(4):
                softmax_batch(NB - 4 + j4, j4 % 2, j4, j4 < 2)
            dve.wait_ge(s["c_den"], upto(NB - 1))
            V.tensor_copy(node_den[:], node_ps).then_inc(s["nden_rdy"], 1)

            PER_D = 4

            def normalise_batch(b, j, slot, ahead):
                c = Chain("dve_d", PER_D * b)
                dve.wait_ge(s["d_ex"], upto(b))
                c.link(V.tensor_tensor(sel[:, j, :, :, :], bank[2 + j][:, 0:B * RH].rearrange("p (b r h) -> p b r h", b=B, r=R),
                                       per_type(tmask, b), ALU.mult))
                dve.sem_inc(s["d_sel"], 1)
                c.link(V.tensor_reduce(tsel[:, j, :, :], sel[:, j, :, :, :].rearrange("p b r h -> p b h r"), AX_X, ALU.add))
                c.link(V.tensor_scalar(tsel[:, j, :, :], tsel[:, j, :, :], 1e-12, None, ALU.add))
                c.link(V.reciprocal(tsel[:, j, :, :], tsel[:, j, :, :]))
                V.tensor_tensor(attn[:, bass.ds(B * b, B), :], prob[:, bass.ds(B * b, B), :], tsel[:, j, :, :], ALU.mult).then_inc(s["dve_turn"], 1)
                if ahead:
                    dve.wait_ge(s["d_ohtp"], upto(b - 2))
                    one_hots(b + 2, (slot + 2) % 4, s["d_oh"])
                assert c.n == PER_D

            one_hots(0, 0, s["d_oh"])
            one_hots(1, 1, s["d_oh"])
            with dve.Fori(0, NB // 4 - 1) as i:
                for j4 in range(4):
                    normalise_batch(4 * i + j4, j4 % 2, j4, True)
            for j4 in range(4):
                normalise_batch(NB - 4 + j4, j4 % 2, j4, j4 < 2)
            dve.wait_ge(s["d_ex"], upto(NB - 1))
            dve.wait_ge(s["d_oht"], upto(NB - 1))
            dve.wait_ge(s["dve_turn"], ROWT + R + 4 + NB)
            V.memset(psum[:, 0:7 * 512], 0.0).then_inc(s["zero2"], 1)

            with dve.Fori(0, NI) as i:
                for j in range(2):
                    b = 2 * i + j
                    dve.wait_ge(s["v_mm"], upto(b - 2))
                    one_hots(b, j, s["dve_v"])
                    dve.wait_ge(s["v0"] if j == 0 else s["v1"], 16 * B * i + 16 * B)
                    V.tensor_tensor(prod[:, j, :, :].rearrange("p b (h d) -> p b h d", h=H), qg[:, j, :, :].rearrange("p b (h d) -> p b h d", h=H),
                                    attn[:, bass.ds(B * b, B), :].unsqueeze(3).broadcast_to((P, B, H, D)), ALU.mult).then_inc(s["wv_ready"], 1)

            dve.wait_ge(s["v_mm"], upto(NB - 1))
            V.tensor_copy(agg[:].rearrange("p t c -> p (t c)"), agg_ps).then_inc(s["agg_rdy"], 1)
            dve.wait_ge(s["s_x"], 32)
            dve.wait_ge(s["s_vecs"], 48)
            for t in range(TILES):
                dve.wait_ge(s["o_mm"], t + 1)
                V.tensor_tensor(hh[:, t, :], bank[2 + t % 2][:, 0:HID], ob_all[:], ALU.add).then_inc(s["o_ev"], 1)
            dve.wait_ge(s["o_ev"], TILES)
            c = Chain("dve_t")

            def bc(v):
                return v.unsqueeze(2).broadcast_to((P, TILES, HID))

            def all_tiles(v):
                return v.unsqueeze(1).broadcast_to((P, TILES, HID))

            def centre_and_scale(n):
                c.link(V.tensor_reduce(mu[:], hh[:], AX_X, ALU.add))
                c.link(V.tensor_scalar(mu[:], mu[:], 1.0 / HID, None, ALU.mult))
                c.link(V.tensor_tensor(hh[:], hh[:], bc(mu[:]), ALU.subtract))
                c.link(V.tensor_tensor(sq[:], hh[:], hh[:], ALU.mult))
                c.link(V.tensor_reduce(var[:], sq[:], AX_X, ALU.add))
                c.link(V.tensor_scalar(var[:], var[:], 1.0 / HID, 1e-5, ALU.mult, ALU.add))
                dve.sem_inc(s["sq_ask"], 1)
                dve.wait_ge(s["sq_got"], n + 1)
                c.link(V.reciprocal(var[:], var[:]))

            c.link(V.tensor_tensor(hh[:], hh[:], x_n[:], ALU.add))
            centre_and_scale(0)
            c.link(V.tensor_tensor(hh[:], hh[:], bc(var[:]), ALU.mult))
            c.link(V.tensor_tensor(hh[:], hh[:], all_tiles(ga_all[:]), ALU.mult))
            c.link(V.tensor_tensor(hh[:], hh[:], all_tiles(be_all[:]), ALU.add))
            c.link(V.tensor_tensor(hh[:], hh[:], x_n[:], ALU.add))
            centre_and_scale(1)
            V.tensor_tensor(sq[:], hh[:], bc(var[:]), ALU.mult).then_inc(s["fin"], 1)


INPUTS = ["x", "src", "dst", "edge_type_5", "L0_gnn_W_Q", "L0_gnn_W_K", "L0_gnn_W_V", "L0_gnn_attn_bias",
          "L0_gnn_out_proj_w", "L0_gnn_out_proj_b", "L0_gnn_ln_gamma", "L0_gnn_ln_beta"]


def kernel(**inputs):
    import numpy as np
    import concourse.bacc as bacc
    from concourse.bass_utils import run_bass_kernel_spmd

    nc = bacc.Bacc("TRN2", target_bir_lowering=False, num_devices=1)
    arrays, args = {}, []
    for name in INPUTS:
        a = np.ascontiguousarray(inputs[name])
        arrays[f"in_{name}_dram"] = a
        args.append(nc.dram_tensor(f"in_{name}_dram", a.shape, mybir.dt.from_np(a.dtype), kind="ExternalInput").ap())
    out = nc.dram_tensor("out_0_dram", inputs["x"].shape, F32, kind="ExternalOutput").ap()
    gnn_layer(nc, *args, out)
    r = run_bass_kernel_spmd(nc, [arrays], core_ids=[0])
    return r.results[0]["out_0_dram"]
```

```python
from contextlib import ExitStack

import concourse.bass as bass
from concourse import mybir

F32 = mybir.dt.float32
BF16 = mybir.dt.bfloat16
I32 = mybir.dt.int32
ALU = mybir.AluOpType
ACT = mybir.ActivationFunctionType
AX_X = mybir.AxisListType.X

P = 128
BIG = 1.0e30


def gnn_layer(nc, x, src, dst, etype, w_q, w_k, w_v, attn_bias, out_w, out_b, gamma, beta, out):
    N, HID = x.shape
    E = src.shape[0]
    R, H, _, D = w_q.shape
    RH = R * H
    TILES = -(-N // P)
    NPAD = TILES * P
    LASTN = N - (TILES - 1) * P
    ROWS = -(-E // P)
    FULL = E // P
    TAIL = E - FULL * P
    B = 4
    STEPS = -(-(ROWS + TILES - 1) // (2 * B)) * 2 * B
    NB = STEPS // B
    NI = NB // 2
    ROWT = -(-STEPS // P)
    RROWS = ROWS + 1
    KW = HID + H
    PERB = 12
    TBANKS = -(-TILES // PERB)
    SCALE = 1.0 / (D ** 0.5)
    DVE_R = list(range(0, R, 2))
    ACT_R = list(range(1, R, 2))
    CPLUS_DONE = 3
    ROWI_DONE = CPLUS_DONE + 5
    ADDR_DONE = ROWI_DONE + 4 + 2 * (TBANKS - 1)
    DLOC_DONE = ADDR_DONE + 7
    SHIFT_DONE = DLOC_DONE + 3
    assert HID == P and H * D == P and 0 < TAIL < P and B * P == 512 and PERB * RH <= 512

    rec = nc.dram_tensor("edge_rows", [RROWS, 3 * P], I32).ap()
    k_tab = nc.dram_tensor("k_table", [NPAD * R, KW], F32).ap()
    v_tab = nc.dram_tensor("v_table", [NPAD * R, HID], F32).ap()
    q_tab = nc.dram_tensor("q_table", [NPAD * R, HID], F32).ap()
    dflat = nc.dram_tensor("local_dst", [1, ROWT * P * P + 2], F32).ap()

    with ExitStack() as ctx:
        def sb(name, shape, dt=F32):
            return ctx.enter_context(nc.sbuf_tensor(name, shape, dt))

        def sem(name):
            return ctx.enter_context(nc.semaphore(name))

        psum = ctx.enter_context(nc.psum_tensor("psum", [P, 8 * 512], F32))
        bank = [psum[:, 512 * n:512 * (n + 1)] for n in range(8)]
        node_ps = psum[:, 5 * 512:8 * 512]
        agg_ps = psum[:, 0:TILES * HID]

        iota_n = sb("iota_n", [P, P])
        iota_i = sb("iota_i", [P, P], I32)
        ident = sb("ident", [P, P])
        ones = sb("ones", [P, P])
        step_id = sb("step_id", [P, ROWT])
        step_i = sb("step_i", [P, ROWT], I32)
        crow_i = sb("crow_i", [1, RROWS], I32)
        pad_row = sb("pad_row", [1, 3 * P], I32)
        neg5 = sb("neg5", [1, 2])
        x_n = sb("x_n", [P, TILES, HID])
        xs = sb("xs", [P, 2, HID])
        xt = sb("xt", [P, 2, P])
        w_all = sb("w_all", [P, R, 3, HID])
        wo_raw = sb("wo_raw", [P, HID])
        wo_t = sb("wo_t", [P, HID])
        ob_all = sb("ob_all", [P, HID])
        ga_all = sb("ga_all", [P, HID])
        be_all = sb("be_all", [P, HID])
        kst = sb("kst", [P, 2, R, KW])
        vst = sb("vst", [P, 2, R, HID])
        qst = sb("qst", [P, 2, R, HID])
        last_i = sb("last_i", [1, RROWS], I32)
        tile_i = sb("tile_i", [1, RROWS], I32)
        crow = sb("crow", [1, RROWS])
        cplus = sb("cplus", [1, RROWS])
        row_f = sb("row_f", [P, ROWT])
        row_i = sb("row_i", [P, ROWT], I32)
        tile_f = sb("tile_f", [P, ROWT])
        ge1 = sb("ge1", [P, ROWT])
        ge2 = sb("ge2", [P, ROWT])
        addr2 = sb("addr2", [P, ROWT, 2])
        addr_row = sb("addr_row", [1, 2, ROWT * P], I32)
        erow = sb("erow", [P, ROWT, 3, P], I32)
        kidx = sb("kidx", [P, ROWT * P])
        qidx = sb("qidx", [P, ROWT * P])
        ety = sb("ety", [P, ROWT * P])
        dloc = sb("dloc", [P, ROWT * P])
        pen = sb("pen", [P, ROWT * P])
        islast = sb("islast", [P, ROWT * P])
        tmask = sb("tmask", [P, STEPS, R])
        tpen = sb("tpen", [P, STEPS, R])
        logit = sb("logit", [P, STEPS, H])
        prob = sb("prob", [P, STEPS, H])
        attn = sb("attn", [P, STEPS, H])
        flat_l, flat_p, flat_a = (t[:].rearrange("p s h -> p (s h)") for t in (logit, prob, attn))
        erf = flat_p[:, 0:6 * ROWT * P].rearrange("p (n k e) -> p n k e", n=6, k=ROWT)
        esf = flat_a[:, 0:3 * ROWT * P].rearrange("p (k n e) -> p k n e", k=ROWT, n=3)
        less = flat_a[:, 3 * ROWT * P:3 * ROWT * P + ROWT * RROWS].rearrange("p (k c) -> p k c", k=ROWT)
        shl = flat_l[:, 0:2 * ROWT * P].rearrange("p (n k e) -> p n k e", n=2, k=ROWT)
        ist = sb("ist", [P, 2, 2, B], I32)
        pst = sb("pst", [P, 2, B])
        ring = sb("ring", [P, 2 * B * (KW + HID)])
        kg = ring[:, 0:2 * B * KW].rearrange("p (j b c) -> p j b c", j=2, b=B)
        qg = ring[:, 2 * B * KW:].rearrange("p (j b c) -> p j b c", j=2, b=B)
        vg = ring[:, 0:4 * B * HID].rearrange("p (j b c) -> p j b c", j=4, b=B)
        prod = sb("prod", [P, 2, B, HID])
        lsum = sb("lsum", [P, 2, B, H])
        ml = sb("ml", [P, 2, B, R, H])
        oh = sb("oh", [P, 4, B, P])
        oht = sb("oht", [P, 2, B, P], BF16)
        pen_s = sb("pen_s", [RH, 2, B * P])
        fwd = sb("fwd", [RH, 2, B * P])
        fe = sb("fe", [P, 2, B, RH])
        sel = sb("sel", [P, 2, B * R, 3 * H])
        tsel = sb("tsel", [P, 2, B, H])
        zed = sb("zed", [P, 2, B, H])
        pm = sb("pm", [P, 2, B, R, H])
        att = sb("att", [P, 2, B, H])
        node_f = sb("node_f", [P, TBANKS * 512])
        node3 = sb("node3", [P, TBANKS * 512 // H, 3, H], BF16)
        agg = logit[:].rearrange("p s h -> p (s h)")[:, 0:TILES * HID].rearrange("p (t c) -> p t c", t=TILES)
        hh = prob[:].rearrange("p s h -> p (s h)")[:, 0:TILES * HID].rearrange("p (t c) -> p t c", t=TILES)
        sq = attn[:].rearrange("p s h -> p (s h)")[:, 0:TILES * HID].rearrange("p (t c) -> p t c", t=TILES)
        agt = sb("agt", [P, 2, P])
        mu = sb("mu", [P, TILES])
        var = sb("var", [P, TILES])

        s = {n: sem(n) for n in (
            "s_x s_xs0 s_xs1 s_w s_wo s_vecs s_bias s_pad s_ip s_rec s_lastd s_const s_id s_wot "
            "sch sch_ps s_erow s_dfl s_shl addr_ps addr_rdy tr_ps tr_sb edges_rdy zero_rdy "
            "xt_ps xt_sb tab_mm tab_dve tab_act tab_out0 tab_out1 "
            "ist_ready pst_ready kq0 kq1 logit_done ml_ready oh_ready mlt_ready pens_ready f_ready fb_ready fe_ready tmax_mm "
            "nmax_rdy dve_b dve_c dve_d dve_v dve_t "
            "c_oh c_ohtp c_oht c_ex c_sel c_z c_p c_pm c_den "
            "nden_rdy zero2 split1 split2 attn_done d_oh d_ohtp d_oht d_ex d_sel "
            "vist_ready v0 v1 v2 v3 wv_ready v_mm agg_rdy "
            "o_tr o_cp o_mm o_ev fin s_out sq_ask sq_got pool_turn act_turn sp_turn pe_turn dve_turn").split()}

        CREDIT = 4

        def upto(b):
            return b + CREDIT + 1

        x_full = x[0:(TILES - 1) * P, :].rearrange("(t p) d -> p t d", p=P)
        out_full = out[0:(TILES - 1) * P, :].rearrange("(t p) d -> p t d", p=P)

        block = ctx.enter_context(nc.Block())

        def addr_of(pe, which, step):
            return pe.value_load(addr_row[0:1, which, bass.ds(step, 1)], min_val=0,
                                 max_val=(TILES - 1) * P if which else (TBANKS - 1) * 512 + PERB * RH)

        @block.sync
        def _(sp):
            sp.wait_ge(s["s_pad"], 2)
            for n, a in enumerate((src, dst, etype)):
                sp.dma_start(rec[0:FULL, n * P:(n + 1) * P], a[0:FULL * P].rearrange("(c e) -> c e", e=P)).then_inc(s["s_rec"], 16)
                sp.dma_start(rec[FULL:FULL + 1, n * P:n * P + TAIL], a[FULL * P:E].rearrange("(c e) -> c e", c=1)).then_inc(s["s_rec"], 16)
                sp.dma_start(rec[FULL:FULL + 1, n * P + TAIL:(n + 1) * P], pad_row[:, n * P + TAIL:(n + 1) * P]).then_inc(s["s_rec"], 16)
            sp.dma_start(rec[ROWS:RROWS, :], pad_row[:, :]).then_inc(s["s_rec"], 16)
            sp.wait_ge(s["s_rec"], 160)
            sp.dma_start(last_i[:], rec.rearrange("c e -> e c")[2 * P - 1:2 * P, :], allow_slow_non_contiguous=True).then_inc(s["s_lastd"], 16)
            sp.wait_ge(s["sch"], DLOC_DONE)
            sp.dma_start(dflat[:, 1:ROWT * P * P + 1].rearrange("o (k p e) -> (o p) k e", k=ROWT, e=P), erf[:, 3, :, :]).then_inc(s["s_dfl"], 16)
            sp.dma_start(dflat[:, 0:1], neg5[:, 0:1]).then_inc(s["s_dfl"], 16)
            sp.dma_start(dflat[:, ROWT * P * P + 1:ROWT * P * P + 2], neg5[:, 1:2]).then_inc(s["s_dfl"], 16)
            sp.wait_ge(s["s_dfl"], 48)
            sp.dma_start(shl[:, 0, :, :], dflat[:, 0:ROWT * P * P].rearrange("o (k p e) -> (o p) k e", k=ROWT, e=P)).then_inc(s["s_shl"], 16)
            sp.dma_start(shl[:, 1, :, :], dflat[:, 2:ROWT * P * P + 2].rearrange("o (k p e) -> (o p) k e", k=ROWT, e=P)).then_inc(s["s_shl"], 16)

            def load_tile(t, j):
                sp.dma_start(xs[:, j, :], x[bass.ds(t * P, P), :]).then_inc(s["s_xs0"] if j == 0 else s["s_xs1"], 16)

            def store_tile(t, j):
                done = s["tab_out0"] if j == 0 else s["tab_out1"]
                sp.wait_ge(s["tab_dve"], len(DVE_R) * (t + 1))
                sp.sem_inc(s["sp_turn"], 1)
                sp.wait_ge(s["tab_act"], len(ACT_R) * (t + 1))
                sp.sem_inc(s["sp_turn"], 1)
                sp.dma_start(k_tab[bass.ds(t * (P * R), P * R), :].rearrange("(p r) c -> p r c", r=R), kst[:, j, :, :]).then_inc(done, 16)
                sp.dma_start(v_tab[bass.ds(t * (P * R), P * R), :].rearrange("(p r) c -> p r c", r=R), vst[:, j, :, :]).then_inc(done, 16)
                sp.dma_start(q_tab[bass.ds(t * (P * R), P * R), :].rearrange("(p r) c -> p r c", r=R), qst[:, j, :, :]).then_inc(done, 16)

            load_tile(0, 0)
            load_tile(1, 1)
            with sp.Fori(0, TILES // 2 - 1) as i:
                for j in range(2):
                    sp.wait_ge(s["xt_ps"], 2 * i + j + 1)
                    sp.sem_inc(s["sp_turn"], 1)
                    load_tile(2 * i + j + 2, j)
                    store_tile(2 * i + j, j)
            sp.wait_ge(s["xt_ps"], TILES - 2)
            sp.dma_start(xs[0:LASTN, 0, :], x[(TILES - 1) * P:N, :]).then_inc(s["s_xs0"], 16)
            for t in range(TILES - 3, TILES):
                store_tile(t, t % 2)
            sp.dma_start(x_n[:, 0:TILES - 1, :], x_full).then_inc(s["s_x"], 16)
            sp.dma_start(x_n[0:LASTN, TILES - 1, :], x[(TILES - 1) * P:N, :]).then_inc(s["s_x"], 16)

            sp.wait_ge(s["fin"], 1)
            sp.dma_start(out_full, sq[:, 0:TILES - 1, :]).then_inc(s["s_out"], 16)
            sp.dma_start(out[(TILES - 1) * P:N, :], sq[0:LASTN, TILES - 1, :]).then_inc(s["s_out"], 16)
            sp.wait_ge(s["s_out"], 32)

        @block.gpsimd
        def _(pool):
            nc.gpsimd.memset(pad_row[:, 0:3 * P], 0).then_inc(s["s_ip"], 1)
            pool.wait_ge(s["s_ip"], 1)
            nc.gpsimd.memset(pad_row[:, P:2 * P], NPAD - 1).then_inc(s["s_pad"], 1)
            nc.gpsimd.memset(neg5[:], -5.0e5).then_inc(s["s_pad"], 1)
            nc.gpsimd.iota(iota_i[:], [[1, P]], base=0, channel_multiplier=0).then_inc(s["s_const"], 1)
            nc.gpsimd.iota(crow_i[:], [[1, RROWS]], base=0, channel_multiplier=0).then_inc(s["s_const"], 1)
            nc.gpsimd.iota(step_i[:], [[P, ROWT]], base=0, channel_multiplier=1).then_inc(s["s_const"], 1)
            nc.gpsimd.memset(ones[:], 1.0).then_inc(s["s_const"], 1)
            nc.gpsimd.memset(ident[:], 0.0).then_inc(s["s_id"], 1)
            pool.wait_ge(s["s_id"], 1)
            nc.gpsimd.affine_select(out=ident[:], in_=ident[:], compare_op=ALU.not_equal, fill=1.0, base=0,
                                    pattern=[[-1, P]], channel_multiplier=1).then_inc(s["s_id"], 1)
            pool.wait_ge(s["s_rec"], 160)
            pool.wait_ge(s["sch"], ROWI_DONE)
            for k in range(ROWT):
                nc.gpsimd.indirect_dma_start(erow[:, k, :, :].rearrange("p a e -> p (a e)"), None, rec,
                                             bass.IndirectOffsetOnAxis(ap=row_i[:, k:k + 1], axis=0)).then_inc(s["s_erow"], 16)
            pool.wait_ge(s["tab_out0"], 48 * (TILES - TILES // 2))
            pool.wait_ge(s["tab_out1"], 48 * (TILES // 2))
            with pool.Fori(0, NI) as i:
                for j in range(2):
                    b = 2 * i + j
                    pool.wait_ge(s["ist_ready"], upto(b))
                    pool.sem_inc(s["pool_turn"], 1)
                    done = s["kq0"] if j == 0 else s["kq1"]
                    for k in range(B):
                        nc.gpsimd.indirect_dma_start(kg[:, j, k, :], None, k_tab, bass.IndirectOffsetOnAxis(ap=ist[:, j, 0, k:k + 1], axis=0)).then_inc(done, 16)
                        nc.gpsimd.indirect_dma_start(qg[:, j, k, :], None, q_tab, bass.IndirectOffsetOnAxis(ap=ist[:, j, 1, k:k + 1], axis=0)).then_inc(done, 16)
            with pool.Fori(0, NB // 4) as i:
                for q in range(4):
                    pool.wait_ge(s["vist_ready"], upto(4 * i + q))
                    pool.sem_inc(s["pool_turn"], 1)
                    for k in range(B):
                        nc.gpsimd.indirect_dma_start(vg[:, q, k, :], None, v_tab,
                                                     bass.IndirectOffsetOnAxis(ap=ist[:, q // 2, q % 2, k:k + 1], axis=0)).then_inc(s[f"v{q}"], 16)

        @block.scalar
        def _(act):
            for name in ("ist_ready", "pst_ready", "pens_ready", "fe_ready", "c_oht", "c_p", "d_oht", "vist_ready"):
                act.sem_inc(s[name], CREDIT)
            for j in range(2):
                for r in range(R):
                    act.dma_start(kst[:, j, r, HID:KW], attn_bias[r:r + 1, :].broadcast_to((P, H))).then_inc(s["s_bias"], 16)
            for n, w in ((0, w_k), (1, w_v), (2, w_q)):
                for r in range(R):
                    act.dma_start(w_all[:, r, n, :].rearrange("k (h d) -> k h d", h=H), w[r].rearrange("h k d -> k h d")).then_inc(s["s_w"], 16)
            act.dma_start(wo_raw[:], out_w).then_inc(s["s_wo"], 16)
            for t, v in ((ob_all, out_b), (ga_all, gamma), (be_all, beta)):
                act.dma_start(t[:], v.rearrange("(a c) -> a c", a=1).broadcast_to((P, HID))).then_inc(s["s_vecs"], 16)

            def table_tile(t, j, free):
                act.wait_ge(s["xt_ps"], t + 1)
                nc.scalar.copy(xt[:, j, :], bank[5 + j][:, 0:P]).then_inc(s["xt_sb"], 1)
                if free is not None:
                    act.wait_ge(*free)
                for r in ACT_R:
                    act.wait_ge(s["tab_mm"], R * t + r + 1)
                    nc.scalar.copy(kst[:, j, r, 0:HID], bank[r][:, 0:HID])
                    nc.scalar.copy(vst[:, j, r, :], bank[r][:, HID:2 * HID])
                    nc.scalar.mul(qst[:, j, r, :], bank[r][:, 2 * HID:3 * HID], SCALE).then_inc(s["tab_act"], 1)

            for t in range(2):
                table_tile(t, t, None)
            with act.Fori(1, TILES // 2) as i:
                for j in range(2):
                    table_tile(2 * i + j, j, (s["tab_out0"] if j == 0 else s["tab_out1"], 48 * i))
            table_tile(TILES - 1, 0, (s["tab_out0"], 48 * (TILES // 2)))

            act.wait_ge(s["edges_rdy"], 1)

            def stage_indices(b, j):
                nc.scalar.copy(ist[:, j, 0, :], kidx[:, bass.ds(B * b, B)])
                nc.scalar.copy(ist[:, j, 1, :], qidx[:, bass.ds(B * b, B)]).then_inc(s["ist_ready"], 1)

            stage_indices(0, 0)
            stage_indices(1, 1)
            with act.Fori(0, NI) as i:
                for j in range(2):
                    b = 2 * i + j
                    act.wait_ge(s["logit_done"], upto(b))
                    act.sem_inc(s["act_turn"], 1)
                    stage_indices(b + 2, j)
                    act.wait_ge(s["mlt_ready"], upto(b - 2))
                    act.sem_inc(s["act_turn"], 1)
                    nc.scalar.copy(pst[:, j, :], pen[:, bass.ds(B * b, B)]).then_inc(s["pst_ready"], 1)
                    act.wait_ge(s["mlt_ready"], upto(b))
                    nc.scalar.copy(pen_s[:, j, :], bank[2 + j][0:RH, :]).then_inc(s["pens_ready"], 1)
                    act.wait_ge(s["tmax_mm"], upto(b - 2))
                    act.wait_ge(s["fb_ready"], upto(b))
                    act.sem_inc(s["act_turn"], 1)
                    for k in range(B):
                        last = nc.scalar.activation(fe[:, j, k, :], bank[4][:, (j * B + k) * RH:(j * B + k + 1) * RH], ACT.Copy,
                                                    scale=islast[:, bass.ds(B * b + k, 1)])
                    last.then_inc(s["fe_ready"], 1)

            def one_hot_back(b, j, ready, done, used):
                act.wait_ge(used, upto(b - 2))
                act.wait_ge(ready, upto(b))
                nc.scalar.copy(oht[:, j, :, :].rearrange("p b n -> p (b n)"), bank[j]).then_inc(done, 1)

            def exponential(b, j):
                act.wait_ge(s["c_z"], upto(b))
                act.sem_inc(s["act_turn"], 1)
                nc.scalar.activation(prob[:, bass.ds(B * b, B), :], zed[:, j, :, :], ACT.Exp).then_inc(s["c_p"], 1)

            one_hot_back(0, 0, s["c_ohtp"], s["c_oht"], s["c_ex"])
            with act.Fori(0, NI - 1) as i:
                for j in range(2):
                    one_hot_back(2 * i + j + 1, 1 - j, s["c_ohtp"], s["c_oht"], s["c_ex"])
                    exponential(2 * i + j, j)
            one_hot_back(NB - 1, 1, s["c_ohtp"], s["c_oht"], s["c_ex"])
            exponential(NB - 2, 0)
            exponential(NB - 1, 1)
            def stage_value_indices(b, q):
                nc.scalar.copy(ist[:, q // 2, q % 2, :], kidx[:, bass.ds(B * b, B)]).then_inc(s["vist_ready"], 1)

            for q in range(2):
                stage_value_indices(q, q)
            with act.Fori(0, NB // 4) as i:
                for q in range(4):
                    b = 4 * i + q
                    act.wait_ge(s["wv_ready"], upto(b - 2))
                    act.sem_inc(s["act_turn"], 1)
                    stage_value_indices(b + 2, (q + 2) % 4)
                    act.wait_ge(s["d_ex"], upto(b - 2))
                    act.wait_ge(s["d_ohtp"], upto(b))
                    nc.scalar.copy(oht[:, q % 2, :, :].rearrange("p b n -> p (b n)"), bank[7]).then_inc(s["d_oht"], 1)
            for t in range(TILES):
                act.wait_ge(s["o_tr"], t + 1)
                if t >= 2:
                    act.wait_ge(s["o_mm"], t - 1)
                nc.scalar.copy(agt[:, t % 2, :], bank[t % 2][:, 0:P]).then_inc(s["o_cp"], 1)
            for n in range(2):
                act.wait_ge(s["sq_ask"], n + 1)
                nc.scalar.activation(var[:], var[:], ACT.Sqrt).then_inc(s["sq_got"], 1)

        @block.tensor
        def _(pe):
            mm = nc.tensor.matmul
            for name in ("mlt_ready", "fb_ready", "tmax_mm", "c_ohtp", "c_ex", "c_den", "d_ohtp", "d_ex", "v_mm"):
                pe.sem_inc(s[name], CREDIT)

            def addrs_of(which, b):
                return nc.values_load_multi_w_load_instructions(
                    addr_row[0:1, which, bass.ds(B * b, B)], engines=[mybir.EngineType.PE], min_val=0,
                    max_val=(TILES - 1) * P if which else TBANKS * 512 - RH, skip_runtime_bounds_check_because="tiles are clamped to TILES - 1 when the schedule is made")[1]

            pe.wait_ge(s["s_id"], 2)
            pe.wait_ge(s["s_wo"], 16)
            nc.tensor.transpose(bank[7][:, 0:P], wo_raw[:], ident[:]).then_inc(s["s_wot"], 1)
            pe.wait_ge(s["s_const"], 4)
            pe.wait_ge(s["sch"], CPLUS_DONE)
            mm(bank[0][:, 0:RROWS], ones[0:1, :], cplus[:], start=True, stop=True).then_inc(s["sch_ps"], 1)
            pe.wait_ge(s["sch"], ADDR_DONE)
            for n in range(2):
                for k in range(ROWT):
                    last = mm(bank[1 + n][0:1, k * P:(k + 1) * P], addr2[:, k, n:n + 1], ident[:], start=True, stop=True)
            last.then_inc(s["addr_ps"], 1)
            for n in range(6):
                if n == 0:
                    pe.wait_ge(s["sch"], DLOC_DONE)
                if n == 4:
                    pe.wait_ge(s["sch"], SHIFT_DONE)
                if n >= 2:
                    pe.wait_ge(s["tr_sb"], n - 1)
                for k in range(ROWT):
                    last = nc.tensor.transpose(bank[3 + n % 2][:, k * P:(k + 1) * P], erf[:, n, k, :], ident[:])
                last.then_inc(s["tr_ps"], 1)

            pe.wait_ge(s["s_w"], 48 * R)
            pe.wait_ge(s["edges_rdy"], 1)

            def table_tile(t, j, loads, first):
                pe.wait_ge(s["s_xs0"] if j == 0 else s["s_xs1"], loads)
                if not first:
                    pe.wait_ge(s["xt_sb"], t)
                nc.tensor.transpose(bank[5 + j][:, 0:P], xs[:, j, :], ident[:]).then_inc(s["xt_ps"], 1)
                pe.wait_ge(s["xt_sb"], t + 1)
                for r in range(R):
                    if not first:
                        if r in DVE_R:
                            pe.wait_ge(s["tab_dve"], len(DVE_R) * t - len(DVE_R) + DVE_R.index(r) + 1)
                        else:
                            pe.wait_ge(s["tab_act"], len(ACT_R) * t - len(ACT_R) + ACT_R.index(r) + 1)
                    mm(bank[r][:, 0:3 * HID], xt[:, j, :], w_all[:, r, :, :].rearrange("k a c -> k (a c)"),
                       start=True, stop=True).then_inc(s["tab_mm"], 1)

            for t in range(2):
                table_tile(t, t, 16, t == 0)
            with pe.Fori(1, TILES // 2) as i:
                for j in range(2):
                    table_tile(2 * i + j, j, 16 * i + 16, False)
            table_tile(TILES - 1, 0, 16 * (TILES // 2 + 1), False)

            pe.wait_ge(s["zero_rdy"], 1)
            with pe.Fori(0, NI) as i:
                for j in range(2):
                    b = 2 * i + j
                    at = addrs_of(0, b)
                    pe.wait_ge(s["pst_ready"], upto(b))
                    pe.wait_ge(s["f_ready"], upto(b - 2))
                    pe.wait_ge(s["ml_ready"], upto(b))
                    pe.sem_inc(s["pe_turn"], 1)
                    for k in range(B):
                        nc.tensor.transpose(bank[j][0:RH, k * P:(k + 1) * P], ml[:, j, k, :, :].rearrange("p r h -> p (r h)"), ident[:])
                    for k in range(B):
                        last = nc.tensor.transpose(bank[2 + j][0:RH, k * P:(k + 1) * P], pst[:, j, k:k + 1].broadcast_to((P, RH)), ident[:])
                    last.then_inc(s["mlt_ready"], 1)
                    pe.wait_ge(s["fe_ready"], upto(b - 2))
                    pe.wait_ge(s["f_ready"], upto(b))
                    pe.sem_inc(s["pe_turn"], 1)
                    for k in range(B):
                        last = nc.tensor.transpose(bank[4][:, (j * B + k) * RH:(j * B + k + 1) * RH], fwd[:, j, k * P:(k + 1) * P], ident[0:RH, 0:RH])
                    last.then_inc(s["fb_ready"], 1)
                    pe.wait_ge(s["oh_ready"], upto(b))
                    pe.wait_ge(s["fe_ready"], upto(b))
                    pe.sem_inc(s["pe_turn"], 1)
                    for k in range(B):
                        last = mm(node_ps[:, bass.ds(at[k], RH)], oh[:, j, k, :], fe[:, j, k, :],
                                  start=False, stop=True, skip_group_check=True)
                    last.then_inc(s["tmax_mm"], 1)

            def turn(b, out_bank, j4, made, turned):
                pe.wait_ge(made, upto(b))
                for k in range(B):
                    last = nc.tensor.transpose(out_bank[:, k * P:(k + 1) * P], oh[:, j4, k, :], ident[:])
                last.then_inc(turned, 1)

            def expand(b, out_bank, j, back, expanded):
                at = addrs_of(0, b)
                pe.wait_ge(back, upto(b))
                pe.sem_inc(s["pe_turn"], 1)
                for k in range(B):
                    last = mm(out_bank[:, 3 * k * RH:3 * (k + 1) * RH], oht[:, j, k, :],
                              node3[:].rearrange("p g n h -> p (g n h)")[:, bass.ds(at[k] * 3, 3 * RH)], start=True, stop=True)
                last.then_inc(expanded, 1)

            def add_up(b, j, j4):
                at = addrs_of(0, b)
                pe.wait_ge(s["c_pm"], upto(b))
                pe.sem_inc(s["pe_turn"], 1)
                for k in range(B):
                    last = mm(node_ps[:, bass.ds(at[k], RH)], oh[:, j4, k, :],
                              pm[:, j, k, :, :].rearrange("p r h -> p (r h)"), start=False, stop=True, skip_group_check=True)
                last.then_inc(s["c_den"], 1)

            pe.wait_ge(s["nmax_rdy"], 1)

            def turn_c(b, q):
                pe.wait_ge(s["c_oht"], upto(b - 2))
                turn(b, bank[q % 2], q % 4, s["c_oh"], s["c_ohtp"])

            def expand_c(b, q):
                pe.wait_ge(s["c_sel"], upto(b - 2))
                expand(b, bank[2 + q % 2], q % 2, s["c_oht"], s["c_ex"])

            turn_c(0, 0)
            expand_c(0, 0)
            turn_c(1, 1)
            expand_c(1, 1)
            with pe.Fori(0, NB // 4 - 1) as i:
                for q in range(4):
                    b = 4 * i + q + 1
                    turn_c(b + 1, q + 2)
                    add_up(b - 1, q % 2, q)
                    expand_c(b + 1, q + 2)
            for b in range(NB - 3, NB - 1):
                turn_c(b + 1, b + 1)
                add_up(b - 1, (b - 1) % 2, (b - 1) % 4)
                expand_c(b + 1, b + 1)
            add_up(NB - 2, 0, 2)
            add_up(NB - 1, 1, 3)

            pe.wait_ge(s["nden_rdy"], 1)

            def turn_and_expand_d(b, q):
                pe.wait_ge(s["d_sel"], upto(b - 1))
                turn(b, bank[7], q, s["d_oh"], s["d_ohtp"])
                expand(b, bank[7], q % 2, s["d_oht"], s["d_ex"])

            def aggregate(b, q):
                at = addrs_of(1, b)
                pe.wait_ge(s["wv_ready"], upto(b))
                pe.sem_inc(s["pe_turn"], 1)
                for k in range(B):
                    last = mm(agg_ps[:, bass.ds(at[k], HID)], oh[:, q, k, :], prod[:, q % 2, k, :],
                              start=False, stop=True, skip_group_check=True)
                last.then_inc(s["v_mm"], 1)

            turn_and_expand_d(0, 0)
            with pe.Fori(0, NB // 4 - 1) as i:
                for q in range(4):
                    turn_and_expand_d(4 * i + q + 1, (q + 1) % 4)
                    aggregate(4 * i + q, q)
            for b in range(NB - 4, NB - 1):
                turn_and_expand_d(b + 1, (b + 1) % 4)
                aggregate(b, b % 4)
            aggregate(NB - 1, 3)

            def project(t):
                pe.wait_ge(s["o_cp"], t + 1)
                if t >= 2:
                    pe.wait_ge(s["o_ev"], t - 1)
                mm(bank[2 + t % 2][:, 0:HID], agt[:, t % 2, :], wo_t[:], start=True, stop=True).then_inc(s["o_mm"], 1)

            pe.wait_ge(s["agg_rdy"], 1)
            for t in range(TILES):
                if t >= 2:
                    pe.wait_ge(s["o_cp"], t - 1)
                nc.tensor.transpose(bank[t % 2][:, 0:P], agg[:, t, :], ident[:]).then_inc(s["o_tr"], 1)
                if t >= 1:
                    project(t - 1)
            project(TILES - 1)

        @block.vector
        def _(dve):
            V = nc.vector
            for name in ("logit_done", "ml_ready", "oh_ready", "f_ready", "c_oh", "c_sel", "c_z", "c_pm", "d_oh", "d_sel", "wv_ready"):
                dve.sem_inc(s[name], CREDIT)

            class Chain:

                def __init__(self, name, base=0):
                    self.sem, self.n, self.base = s[name], 0, base

                def link(self, ins):
                    self.n += 1
                    ins.then_inc(self.sem, 1)
                    dve.wait_ge(self.sem, self.base + self.n)

            sch = Chain("sch")
            dve.wait_ge(s["s_const"], 4)
            dve.wait_ge(s["s_lastd"], 16)
            sch.link(V.tensor_scalar(tile_i[:], last_i[:], 7, None, ALU.logical_shift_right))
            sch.link(V.tensor_copy(crow[:], crow_i[:]))
            sch.link(V.tensor_tensor(cplus[:], tile_i[:], crow[:], ALU.add))
            assert sch.n == CPLUS_DONE
            sch.link(V.tensor_copy(step_id[:], step_i[:]))
            sch.link(V.tensor_copy(iota_n[:], iota_i[:]))
            dve.wait_ge(s["sch_ps"], 1)
            for k in range(ROWT):
                V.tensor_scalar(less[:, k, :], bank[0][:, 0:RROWS], step_id[:, k:k + 1], None, ALU.is_lt).then_inc(s["dve_turn"], 1)
            dve.wait_ge(s["dve_turn"], ROWT)
            sch.link(V.tensor_reduce(row_f[:], less[:], AX_X, ALU.add))
            sch.link(V.tensor_scalar(row_f[:], row_f[:], float(ROWS), None, ALU.min))
            sch.link(V.tensor_copy(row_i[:], row_f[:]))
            assert sch.n == ROWI_DONE
            sch.link(V.tensor_tensor(tile_f[:], step_id[:], row_f[:], ALU.subtract))
            sch.link(V.tensor_scalar(tile_f[:], tile_f[:], float(TILES - 1), None, ALU.min))
            sch.link(V.tensor_scalar(addr2[:, :, 0], tile_f[:], float(RH), None, ALU.mult))
            for m in range(1, TBANKS):
                sch.link(V.tensor_scalar(ge1[:], tile_f[:], float(PERB * m), float(512 - PERB * RH), ALU.is_ge, ALU.mult))
                sch.link(V.tensor_tensor(addr2[:, :, 0], addr2[:, :, 0], ge1[:], ALU.add))
            sch.link(V.tensor_scalar(addr2[:, :, 1], tile_f[:], float(P), None, ALU.mult))
            assert sch.n == ADDR_DONE
            dve.wait_ge(s["addr_ps"], 1)
            V.tensor_copy(addr_row[:, 0, :], bank[1][0:1, :]).then_inc(s["addr_rdy"], 1)
            V.tensor_copy(addr_row[:, 1, :], bank[2][0:1, :]).then_inc(s["addr_rdy"], 1)
            dve.wait_ge(s["s_erow"], 16 * ROWT)
            sch.link(V.tensor_copy(esf[:], erow[:]))
            sch.link(V.tensor_scalar(erf[:, 0, :, :], esf[:, :, 0, :], float(R), None, ALU.mult))
            sch.link(V.tensor_tensor(erf[:, 0, :, :], erf[:, 0, :, :], esf[:, :, 2, :], ALU.add))
            sch.link(V.tensor_scalar(erf[:, 1, :, :], esf[:, :, 1, :], float(R), None, ALU.mult))
            sch.link(V.tensor_tensor(erf[:, 1, :, :], erf[:, 1, :, :], esf[:, :, 2, :], ALU.add))
            sch.link(V.tensor_copy(erf[:, 2, :, :], esf[:, :, 2, :]))
            sch.link(V.tensor_tensor(erf[:, 3, :, :], esf[:, :, 1, :], addr2[:, :, 1:2].broadcast_to((P, ROWT, P)), ALU.subtract))
            assert sch.n == DLOC_DONE
            dve.wait_ge(s["s_shl"], 32)
            sch.link(V.tensor_tensor(erf[:, 4, :, :], erf[:, 3, :, :], shl[:, 0, :, :], ALU.not_equal))
            sch.link(V.tensor_scalar(erf[:, 4, :, :], erf[:, 4, :, :], -BIG, None, ALU.mult))
            sch.link(V.tensor_tensor(erf[:, 5, :, :], erf[:, 3, :, :], shl[:, 1, :, :], ALU.not_equal))
            assert sch.n == SHIFT_DONE
            for n, t in enumerate((kidx, qidx, ety, dloc, pen, islast)):
                dve.wait_ge(s["tr_ps"], n + 1)
                V.tensor_copy(t[:], bank[3 + n % 2]).then_inc(s["tr_sb"], 1)
            dve.wait_ge(s["tr_sb"], 6)
            for r in range(R):
                V.tensor_scalar(tmask[:, :, r], ety[:, 0:STEPS], float(r), None, ALU.is_equal).then_inc(s["dve_turn"], 1)
            dve.wait_ge(s["dve_turn"], ROWT + R)
            V.tensor_scalar(tpen[:], tmask[:], 1.0, BIG, ALU.subtract, ALU.mult).then_inc(s["edges_rdy"], 1)
            dve.wait_ge(s["s_wot"], 1)
            V.tensor_copy(wo_t[:], bank[7][:, 0:P]).then_inc(s["dve_turn"], 1)
            V.memset(fwd[:, 1, B * P - 1:B * P], -BIG).then_inc(s["dve_turn"], 1)
            V.memset(x_n[:, TILES - 1, :], 0.0).then_inc(s["dve_turn"], 1)

            dve.wait_ge(s["s_bias"], 32 * R)

            def table_tile(t, j, free):
                if free is not None:
                    dve.wait_ge(*free)
                for r in DVE_R:
                    dve.wait_ge(s["tab_mm"], R * t + r + 1)
                    V.tensor_copy(kst[:, j, r, 0:HID], bank[r][:, 0:HID])
                    V.tensor_copy(vst[:, j, r, :], bank[r][:, HID:2 * HID])
                    V.tensor_scalar(qst[:, j, r, :], bank[r][:, 2 * HID:3 * HID], SCALE, None, ALU.mult).then_inc(s["tab_dve"], 1)

            for t in range(2):
                table_tile(t, t, None)
            with dve.Fori(1, TILES // 2) as i:
                for j in range(2):
                    table_tile(2 * i + j, j, (s["tab_out0"] if j == 0 else s["tab_out1"], 48 * i))
            table_tile(TILES - 1, 0, (s["tab_out0"], 48 * (TILES // 2)))
            V.memset(node_ps, 0.0).then_inc(s["zero_rdy"], 1)

            def one_hots(b, slot, done):
                for k in range(B):
                    last = V.tensor_scalar(oh[:, slot, k, :], iota_n[:], dloc[:, bass.ds(B * b + k, 1)], None, ALU.is_equal)
                last.then_inc(done, 1)

            def per_type(t, b):
                return t[:, bass.ds(B * b, B), :].unsqueeze(3).broadcast_to((P, B, R, H))

            PER_B = 3
            with dve.Fori(0, NI) as i:
                for j in range(2):
                    b = 2 * i + j
                    c = Chain("dve_b", PER_B * b)
                    dve.wait_ge(s["kq0"] if j == 0 else s["kq1"], 32 * B * i + 32 * B)
                    c.link(V.tensor_tensor(prod[:, j, :, :], kg[:, j, :, 0:HID], qg[:, j, :, :], ALU.mult))
                    c.link(V.tensor_reduce(lsum[:, j, :, :], prod[:, j, :, :].rearrange("p b (h d) -> p b h d", h=H), AX_X, ALU.add))
                    V.tensor_tensor(logit[:, bass.ds(B * b, B), :], lsum[:, j, :, :], kg[:, j, :, HID:KW], ALU.add).then_inc(s["logit_done"], 1)
                    dve.wait_ge(s["tmax_mm"], upto(b - 2))
                    dve.wait_ge(s["logit_done"], upto(b))
                    c.link(V.tensor_tensor(ml[:, j, :, :, :], logit[:, bass.ds(B * b, B), :].unsqueeze(2).broadcast_to((P, B, R, H)),
                                           per_type(tmask, b), ALU.mult))
                    V.tensor_tensor(ml[:, j, :, :, :], ml[:, j, :, :, :], per_type(tpen, b), ALU.add).then_inc(s["ml_ready"], 1)
                    one_hots(b, j, s["oh_ready"])
                    dve.wait_ge(s["f_ready"], upto(b - 1))
                    dve.wait_ge(s["mlt_ready"], upto(b))
                    dve.wait_ge(s["pens_ready"], upto(b))
                    V.tensor_tensor_scan(fwd[:, j, :], pen_s[:, j, :], bank[j][0:RH, :], fwd[:, 1 - j, B * P - 1:B * P],
                                         ALU.add, ALU.max).then_inc(s["f_ready"], 1)
                    assert c.n == PER_B

            def split_nodes(tag):
                c = Chain(tag)
                f = node_f[:].rearrange("p (g h) -> p g h", h=H)
                c.link(V.tensor_copy(node_f[:], node_ps))
                c.link(V.tensor_copy(node3[:, :, 0, :], f))
                c.link(V.tensor_tensor(f, f, node3[:, :, 0, :], ALU.subtract))
                c.link(V.tensor_copy(node3[:, :, 1, :], f))
                c.link(V.tensor_tensor(f, f, node3[:, :, 1, :], ALU.subtract))
                c.link(V.tensor_copy(node3[:, :, 2, :], f))

            def pick_type(c, b, j, src_bank, expanded, taken):
                dve.wait_ge(expanded, upto(b))
                c.link(V.tensor_tensor(sel[:, j, :, :], src_bank[:, 0:3 * B * RH].rearrange("p (g n) -> p g n", n=3 * H),
                                       tmask[:].rearrange("p s r -> p (s r)")[:, bass.ds(B * R * b, B * R)].unsqueeze(2).broadcast_to((P, B * R, 3 * H)),
                                       ALU.mult))
                dve.sem_inc(taken, 1)
                c.link(V.tensor_reduce(tsel[:, j, :, :], sel[:, j, :, :].rearrange("p (b r) (n h) -> p b h (r n)", b=B, h=H), AX_X, ALU.add))

            dve.wait_ge(s["tmax_mm"], upto(NB - 1))
            split_nodes("split1")
            V.memset(node_ps, 0.0).then_inc(s["nmax_rdy"], 1)
            PER_C = 3

            def softmax_batch(b, j, slot, ahead):
                c = Chain("dve_c", PER_C * b)
                pick_type(c, b, j, bank[2 + j], s["c_ex"], s["c_sel"])
                c.link(V.tensor_tensor(zed[:, j, :, :], logit[:, bass.ds(B * b, B), :], tsel[:, j, :, :], ALU.subtract))
                V.tensor_scalar(zed[:, j, :, :], zed[:, j, :, :], 0.0, None, ALU.min).then_inc(s["c_z"], 1)
                dve.wait_ge(s["c_den"], upto(b - 2))
                if ahead:
                    one_hots(b + 2, (slot + 2) % 4, s["c_oh"])
                dve.wait_ge(s["c_p"], upto(b))
                V.tensor_tensor(pm[:, j, :, :, :], prob[:, bass.ds(B * b, B), :].unsqueeze(2).broadcast_to((P, B, R, H)),
                                per_type(tmask, b), ALU.mult).then_inc(s["c_pm"], 1)
                assert c.n == PER_C

            one_hots(0, 0, s["c_oh"])
            one_hots(1, 1, s["c_oh"])
            with dve.Fori(0, NB // 4 - 1) as i:
                for j4 in range(4):
                    softmax_batch(4 * i + j4, j4 % 2, j4, True)
            for j4 in range(4):
                softmax_batch(NB - 4 + j4, j4 % 2, j4, j4 < 2)
            dve.wait_ge(s["c_den"], upto(NB - 1))
            split_nodes("split2")
            V.memset(psum[:, 0:7 * 512], 0.0).then_inc(s["nden_rdy"], 1)

            PER_D = 5

            def value_batch(b, j, slot, ahead, landed):
                c = Chain("dve_d", PER_D * b)
                pick_type(c, b, j, bank[7], s["d_ex"], s["d_sel"])
                c.link(V.tensor_scalar(tsel[:, j, :, :], tsel[:, j, :, :], 1e-12, None, ALU.add))
                c.link(V.reciprocal(tsel[:, j, :, :], tsel[:, j, :, :]))
                c.link(V.tensor_tensor(att[:, j, :, :], prob[:, bass.ds(B * b, B), :], tsel[:, j, :, :], ALU.mult))
                dve.wait_ge(s["v_mm"], upto(b - 2))
                dve.wait_ge(s[f"v{slot}"], landed)
                V.tensor_tensor(prod[:, j, :, :].rearrange("p b (h d) -> p (b h) d", h=H), vg[:, slot, :, :].rearrange("p b (h d) -> p (b h) d", h=H),
                                att[:, j, :, :].rearrange("p b h -> p (b h)").unsqueeze(2).broadcast_to((P, B * H, D)), ALU.mult).then_inc(s["wv_ready"], 1)
                if ahead:
                    one_hots(b + 2, (slot + 2) % 4, s["d_oh"])
                assert c.n == PER_D

            one_hots(0, 0, s["d_oh"])
            one_hots(1, 1, s["d_oh"])
            with dve.Fori(0, NB // 4 - 1) as i:
                for j4 in range(4):
                    value_batch(4 * i + j4, j4 % 2, j4, True, 16 * B * i + 16 * B)
            for j4 in range(4):
                value_batch(NB - 4 + j4, j4 % 2, j4, j4 < 2, 16 * B * (NB // 4))

            dve.wait_ge(s["v_mm"], upto(NB - 1))
            V.tensor_copy(agg[:].rearrange("p t c -> p (t c)"), agg_ps).then_inc(s["agg_rdy"], 1)
            dve.wait_ge(s["s_x"], 32)
            dve.wait_ge(s["s_vecs"], 48)
            for t in range(TILES):
                dve.wait_ge(s["o_mm"], t + 1)
                V.tensor_tensor(hh[:, t, :], bank[2 + t % 2][:, 0:HID], ob_all[:], ALU.add).then_inc(s["o_ev"], 1)
            dve.wait_ge(s["o_ev"], TILES)
            c = Chain("dve_t")

            def bc(v):
                return v.unsqueeze(2).broadcast_to((P, TILES, HID))

            def all_tiles(v):
                return v.unsqueeze(1).broadcast_to((P, TILES, HID))

            def centre_and_scale(n):
                c.link(V.tensor_reduce(mu[:], hh[:], AX_X, ALU.add))
                c.link(V.tensor_scalar(mu[:], mu[:], 1.0 / HID, None, ALU.mult))
                c.link(V.tensor_tensor(hh[:], hh[:], bc(mu[:]), ALU.subtract))
                c.link(V.tensor_tensor(sq[:], hh[:], hh[:], ALU.mult))
                c.link(V.tensor_reduce(var[:], sq[:], AX_X, ALU.add))
                c.link(V.tensor_scalar(var[:], var[:], 1.0 / HID, 1e-5, ALU.mult, ALU.add))
                dve.sem_inc(s["sq_ask"], 1)
                dve.wait_ge(s["sq_got"], n + 1)
                c.link(V.reciprocal(var[:], var[:]))

            c.link(V.tensor_tensor(hh[:], hh[:], x_n[:], ALU.add))
            centre_and_scale(0)
            c.link(V.tensor_tensor(hh[:], hh[:], bc(var[:]), ALU.mult))
            c.link(V.tensor_tensor(hh[:], hh[:], all_tiles(ga_all[:]), ALU.mult))
            c.link(V.tensor_tensor(hh[:], hh[:], all_tiles(be_all[:]), ALU.add))
            c.link(V.tensor_tensor(hh[:], hh[:], x_n[:], ALU.add))
            centre_and_scale(1)
            V.tensor_tensor(sq[:], hh[:], bc(var[:]), ALU.mult).then_inc(s["fin"], 1)


INPUTS = ["x", "src", "dst", "edge_type_5", "L0_gnn_W_Q", "L0_gnn_W_K", "L0_gnn_W_V", "L0_gnn_attn_bias",
          "L0_gnn_out_proj_w", "L0_gnn_out_proj_b", "L0_gnn_ln_gamma", "L0_gnn_ln_beta"]


def kernel(**inputs):
    import numpy as np
    import concourse.bacc as bacc
    from concourse.bass_utils import run_bass_kernel_spmd

    nc = bacc.Bacc("TRN2", target_bir_lowering=False, num_devices=1)
    arrays, args = {}, []
    for name in INPUTS:
        a = np.ascontiguousarray(inputs[name])
        arrays[f"in_{name}_dram"] = a
        args.append(nc.dram_tensor(f"in_{name}_dram", a.shape, mybir.dt.from_np(a.dtype), kind="ExternalInput").ap())
    out = nc.dram_tensor("out_0_dram", inputs["x"].shape, F32, kind="ExternalOutput").ap()
    gnn_layer(nc, *args, out)
    r = run_bass_kernel_spmd(nc, [arrays], core_ids=[0])
    return r.results[0]["out_0_dram"]
```

```python
from contextlib import ExitStack

import concourse.bass as bass
from concourse import mybir

F32 = mybir.dt.float32
BF16 = mybir.dt.bfloat16
I32 = mybir.dt.int32
ALU = mybir.AluOpType
ACT = mybir.ActivationFunctionType
AX_X = mybir.AxisListType.X

P = 128
BIG = 1.0e30


def gnn_layer(nc, x, src, dst, etype, w_q, w_k, w_v, attn_bias, out_w, out_b, gamma, beta, out):
    N, HID = x.shape
    E = src.shape[0]
    R, H, _, D = w_q.shape
    RH = R * H
    KW = HID + H
    TILES = -(-N // P)
    NPAD = TILES * P
    LASTN = N - (TILES - 1) * P
    ROWS = -(-E // P)
    FULL = E // P
    TAIL = E - FULL * P
    B = 4
    STEPS = -(-(ROWS + TILES - 1) // (2 * B)) * 2 * B
    NB = STEPS // B
    NI = NB // 2
    ROWT = -(-STEPS // P)
    RROWS = ROWS + 1
    LAG = TILES + 1
    SPAN = B * (LAG - 3) - (B - 1)
    V_SLOT = (0, 1, 2, 3, 0, 1, 2)
    GROUPS = [range(g, min(g + B, TILES)) for g in range(0, TILES, B)]
    HALF_G = len(GROUPS) // 2 + 1
    WIN = B * RH
    KQ_SCALE = 1.0 / D ** 0.25
    EARLY0, EARLY1, EARLY2, EARLY3 = 2, 4, 8, 12
    CPLUS_DONE = 3
    ROWI_DONE = CPLUS_DONE + 5
    ADDR_DONE = ROWI_DONE + 4
    DLOC_DONE = ADDR_DONE + 7
    SHIFT_DONE = DLOC_DONE + 3
    CHK_P = max(p for p in range(1, P + 1) if E % p == 0)
    CHK_C = E // CHK_P
    assert CHK_C + 10 <= ROWT * 3 * P
    assert HID == P and H * D == P and 0 < TAIL < P and B * P == 512
    assert LAG % 4 == 2 and NB % 8 == 0 and SPAN + 1 < STEPS

    rec = nc.dram_tensor("edge_rows", [RROWS, 3 * P], I32).ap()
    srt = nc.dram_tensor("sorted_edge_rows", [ROWS, 3 * P], I32).ap()
    k_tab = nc.dram_tensor("k_table", [NPAD * R, KW], F32).ap()
    v_tab = nc.dram_tensor("v_table", [NPAD * R, HID], F32).ap()
    q_tab = nc.dram_tensor("q_table", [NPAD * R, HID], F32).ap()
    dflat = nc.dram_tensor("local_dst", [1, ROWT * P * P + 2], F32).ap()
    pen_rows = nc.dram_tensor("run_penalty", [1, ROWT * P * P], F32).ap()

    with ExitStack() as ctx:
        def sb(name, shape, dt=F32):
            return ctx.enter_context(nc.sbuf_tensor(name, shape, dt))

        def sem(name):
            return ctx.enter_context(nc.semaphore(name))

        psum = ctx.enter_context(nc.psum_tensor("psum", [P, 8 * 512], F32))
        bank = [psum[:, 512 * n:512 * (n + 1)] for n in range(8)]
        ml_ps, back_ps, win_t = (bank[0], bank[1]), bank[2], bank[3][:, 0:WIN]
        v_ps = [psum[:, 512 * n:512 * n + R * HID] for n in (4, 6)]
        turn_ps, exp_ps, win_d = (bank[4], bank[5]), bank[6], bank[7][:, 0:WIN]
        agg_ps = psum[:, 0:TILES * HID]

        iota_n = sb("iota_n", [P, P])
        iota_i = sb("iota_i", [P, P], I32)
        ident = sb("ident", [P, P])
        ones = sb("ones", [P, P])
        step_id = sb("step_id", [P, ROWT])
        step_i = sb("step_i", [P, ROWT], I32)
        crow_i = sb("crow_i", [1, RROWS], I32)
        pad_row = sb("pad_row", [1, 3 * P], I32)
        neg5 = sb("neg5", [1, 2])
        x_n = sb("x_n", [P, TILES, HID])
        xt_all = x_n
        xs = sb("xs", [P, 2, HID])
        xt = sb("xt", [P, 2, P])
        w_kq = sb("w_kq", [P, 2, R, HID])
        w_val = sb("w_val", [P, R, HID])
        wo_raw = sb("wo_raw", [P, HID])
        wo_t = sb("wo_t", [P, HID])
        ob_all = sb("ob_all", [P, HID])
        ga_all = sb("ga_all", [P, HID])
        be_all = sb("be_all", [P, HID])
        stage = sb("stage", [P, 4 * R * KW + 2 * R * HID])
        kqst = stage[:, 0:4 * R * KW].rearrange("p (j r a c) -> p j r a c", j=2, r=R, a=2)
        vst = stage[:, 4 * R * KW:].rearrange("p (j c) -> p j c", j=2)
        last_i = sb("last_i", [1, RROWS], I32)
        tile_i = sb("tile_i", [1, RROWS], I32)
        crow = sb("crow", [1, RROWS])
        cplus = sb("cplus", [1, RROWS])
        row_f = sb("row_f", [P, ROWT])
        row_i = sb("row_i", [P, ROWT], I32)
        tile_f = sb("tile_f", [P, ROWT])
        addr2 = sb("addr2", [P, ROWT, 2])
        addr_row = sb("addr_row", [1, 2, ROWT * P], I32)
        rel_row = sb("rel_row", [1, STEPS], I32)
        acc_row = sb("acc_row", [1, NB + 1], I32)
        spans = sb("spans", [1, STEPS - SPAN - 1])
        long_i = sb("long_i", [1, 2], I32)
        zeros = sb("zeros", [1, WIN], BF16)
        erow = sb("erow", [P, ROWT, 3, P], I32)
        kidx = sb("kidx", [P, ROWT * P])
        qidx = sb("qidx", [P, ROWT * P])
        ety = sb("ety", [P, ROWT * P])
        dloc = sb("dloc", [P, ROWT * P])
        islast = sb("islast", [P, ROWT * P])
        neg_dloc = islast
        tmask = sb("tmask", [P, STEPS, R])
        tpen = sb("tpen", [P, STEPS, R])
        logit = sb("logit", [P, STEPS, H])
        prob = sb("prob", [P, STEPS, H])
        work = sb("work", [P, 2 * B * (KW + HID) + 2 * B * HID + 4 * B * P])
        flat_l, flat_p = (t[:].rearrange("p s h -> p (s h)") for t in (logit, prob))
        flat_a = work[:]
        erf = flat_p[:, 0:6 * ROWT * P].rearrange("p (n k e) -> p n k e", n=6, k=ROWT)
        esf = flat_a[:, 0:3 * ROWT * P].rearrange("p (k n e) -> p k n e", k=ROWT, n=3)
        less = flat_a[:, 3 * ROWT * P:3 * ROWT * P + ROWT * RROWS].rearrange("p (k c) -> p k c", k=ROWT)
        shl = flat_l[:, 0:2 * ROWT * P].rearrange("p (n k e) -> p n k e", n=2, k=ROWT)
        ints = erow[:].rearrange("p k a e -> p (k a e)")
        chk = ints[0:CHK_P, 0:CHK_C + 1]
        edge3 = ints[:, CHK_C + 1:CHK_C + 4]
        spot = ints[:, CHK_C + 4:CHK_C + 7]
        falls = flat_l[0:CHK_P, 0:CHK_C]
        fell = sb("fell", [P, 1])
        unsorted_i = sb("unsorted_i", [1, 1], I32)
        oh_lo, oh_lo_t, dst_rep, same, below, above = (flat_a[:, n * P:(n + 1) * P] for n in range(6))
        count, prefix, start, oh_hi, here = (flat_l[:, n * TILES:(n + 1) * TILES] for n in range(5))
        dst_f, lo_f, hi_f, before, rank, spot_f = (flat_l[:, 5 * TILES + n:5 * TILES + n + 1] for n in range(6))
        lo_i, hi_i, rank_i = (ints[:, CHK_C + 7 + n:CHK_C + 8 + n] for n in range(3))
        ist = sb("ist", [P, 2, 2, B], I32)
        ring = work[:, 0:2 * B * (KW + HID)]
        kg = ring[:, 0:2 * B * KW].rearrange("p (j b c) -> p j b c", j=2, b=B)
        qg = ring[:, 2 * B * KW:].rearrange("p (j b c) -> p j b c", j=2, b=B)
        vg = ring[:, 0:4 * B * HID].rearrange("p (j b c) -> p j b c", j=4, b=B)
        prod = work[:, 2 * B * (KW + HID):2 * B * (KW + 2 * HID)].rearrange("p (j b c) -> p j b c", j=2, b=B)
        v_ahead = sb("v_ahead", [P, NB // 8, B, HID])
        i_ahead = sb("i_ahead", [P, NB // 8, B], I32)
        lsum = sb("lsum", [P, 2, B, H])
        ml = sb("ml", [P, 2, B, R, H])
        oh = work[:, 2 * B * (KW + 2 * HID):].rearrange("p (j b n) -> p j b n", j=4, b=B)
        oht = sb("oht", [P, 2, B, P])
        oht_v = sb("oht_v", [P, 2, B, P], BF16)
        pen_s = sb("pen_s", [RH, 2, B * P])
        fwd = sb("fwd", [RH, 2, B * P])
        fe = sb("fe", [P, 2, B, RH])
        sel3 = sb("sel3", [P, 2, B * R, 3 * H])
        sel = sb("sel", [P, 2, B * R, H])
        tsel = sb("tsel", [P, 2, B, H])
        zed = sb("zed", [P, 2, B, H])
        pm = sb("pm", [P, 2, B, R, H])
        att = sb("att", [P, 2, B, H])
        node_max = sb("node_max", [P, (TILES + B - 1) * RH])
        node_sum = sb("node_sum", [P, (TILES + B - 1) * RH])
        node3 = sb("node3", [P, TILES * R, 3, H], BF16)
        agg = logit[:].rearrange("p s h -> p (s h)")[:, 0:TILES * HID].rearrange("p (t c) -> p t c", t=TILES)
        hh = prob[:].rearrange("p s h -> p (s h)")[:, 0:TILES * HID].rearrange("p (t c) -> p t c", t=TILES)
        sq = work[:, 0:TILES * HID].rearrange("p (t c) -> p t c", t=TILES)
        x_beta = stage[:, 0:TILES * HID].rearrange("p (t c) -> p t c", t=TILES)
        agt = oht
        neg_mu = sb("neg_mu", [P, 2, TILES])
        rstd = sb("rstd", [P, 2, TILES])

        s = {n: sem(n) for n in (
            "s_x s_xs0 s_xs1 s_w s_wv s_wo s_vecs s_bias s_pad s_ip s_rec s_lastd s_const s_id s_wot wo_in "
            "s_chk chk_done fell_ps flag_rdy in_order sort_mask sort_in sort_dve sort_oh sort_zero sort_cnt sort_add sort_base sort_start "
            "sort_t sort_tc sort_rk sort_spot sort_out sort_placed sort_back "
            "sch sch_ps s_erow s_dfl s_shl s_prow pen0 pen1 addr_ps addr_rdy tr_ps tr_sb edges_rdy zero_rdy "
            "xt_ps xt_sb tab_mm tab_act tab_out0 tab_out1 v_in v_mul v_out vst0 vst1 x_room "
            "ist_ready kq0 kq1 logit_done ml_ready oh_ready mlt_ready f_ready fb_ready fe_ready tmax_mm "
            "long_rdy t_acc d_acc win_zero dve_b dve_c dve_d nd_rdy d_abs dve_t "
            "c_oh c_ohtp c_oht c_ex c_sel c_z c_p c_pm c_den "
            "nden_rdy split d_oh d_ohtp d_oht d_ex d_sel "
            "vist_ready i_ahead v0 v1 v2 v3 v_ahead wv_ready v_mm agg_rdy agg_act x_sums "
            "o_tr o_cp o_mm mu_rdy var_rdy fin s_out sq_ask sq_got pool_turn act_turn sp_turn pe_turn dve_turn").split()}

        CREDIT = 4

        def upto(b):
            return b + CREDIT + 1

        x_full = x[0:(TILES - 1) * P, :].rearrange("(t p) d -> p t d", p=P)

        block = ctx.enter_context(nc.Block())

        def pairs(engine, first, end, batch):
            with engine.Fori(first // 2, end // 2) as i:
                for j in range(2):
                    batch(2 * i + j, j)

        def end_slot(b):
            return (2, 0, 1, 3)[b % 4]

        def fours(engine, batch):
            with engine.Fori(0, (LAG - 2) // 4) as i:
                for q in range(4):
                    batch(4 * i + q + NB - LAG, q)

        def short_of(engine):
            return engine.value_load(long_i[0:1, 1:2], min_val=0, max_val=1)

        def long_of(engine):
            return engine.value_load(long_i[0:1, 0:1], min_val=0, max_val=1)

        @block.sync
        def _(sp):
            def store_tile(t, j):
                done = s["tab_out0"] if j == 0 else s["tab_out1"]
                sp.wait_ge(s["tab_act"], R * (t + 1))
                sp.sem_inc(s["sp_turn"], 1)
                sp.dma_start(k_tab[bass.ds(t * (P * R), P * R), :].rearrange("(p r) c -> p r c", r=R), kqst[:, j, :, 0, :]).then_inc(done, 16)
                sp.dma_start(q_tab[bass.ds(t * (P * R), P * R), :].rearrange("(p r) c -> p r c", r=R), kqst[:, j, :, 1, 0:HID]).then_inc(done, 16)

            def early(first, end):
                with sp.Fori(first // 2, end // 2) as i:
                    for j in range(2):
                        store_tile(2 * i + j, j)

            for t in range(2):
                sp.dma_start(xs[:, t, :], x[t * P:(t + 1) * P, :]).then_inc(s[f"s_xs{t}"], 16)
            sp.dma_start(chk[:, 0:CHK_C], dst.rearrange("(p c) -> p c", p=CHK_P)).then_inc(s["s_chk"], 16)
            sp.dma_start(chk[0:CHK_P - 1, CHK_C:CHK_C + 1], dst[CHK_C:E].rearrange("(p c) -> p c", c=CHK_C)[:, 0:1],
                         allow_slow_non_contiguous=True).then_inc(s["s_chk"], 16)
            sp.dma_start(chk[CHK_P - 1:CHK_P, CHK_C:CHK_C + 1], dst[E - 1:E].rearrange("(p c) -> p c", p=1)).then_inc(s["s_chk"], 16)
            sp.wait_ge(s["s_pad"], 2)
            for n, a in enumerate((src, dst, etype)):
                sp.dma_start(rec[0:FULL, n * P:(n + 1) * P], a[0:FULL * P].rearrange("(c e) -> c e", e=P)).then_inc(s["s_rec"], 16)
                sp.dma_start(rec[FULL:FULL + 1, n * P:n * P + TAIL], a[FULL * P:E].rearrange("(c e) -> c e", c=1)).then_inc(s["s_rec"], 16)
                sp.dma_start(rec[FULL:FULL + 1, n * P + TAIL:(n + 1) * P], pad_row[:, n * P + TAIL:(n + 1) * P]).then_inc(s["s_rec"], 16)
            sp.dma_start(rec[ROWS:RROWS, :], pad_row[:, :]).then_inc(s["s_rec"], 16)
            sp.wait_ge(s["s_rec"], 160)
            sp.wait_ge(s["flag_rdy"], 1)
            with sp.If(sp.value_load(unsorted_i[0:1, 0:1], min_val=0, max_val=1) > 0):
                with sp.Fori(0, ROWS) as n:
                    sp.wait_ge(s["sort_add"], n + 1)
                    sp.sem_inc(s["sp_turn"], 1)
                    sp.dma_start(edge3, rec[bass.ds(n, 1), :].rearrange("c (a e) -> e (c a)", a=3), allow_slow_non_contiguous=True).then_inc(s["sort_in"], 16)
                sp.wait_ge(s["sort_add"], ROWS + 1)
                with sp.Fori(0, ROWS) as n:
                    sp.wait_ge(s["sort_placed"], n + 1)
                    sp.sem_inc(s["sp_turn"], 1)
                    sp.dma_start(edge3, rec[bass.ds(n, 1), :].rearrange("c (a e) -> e (c a)", a=3), allow_slow_non_contiguous=True).then_inc(s["sort_in"], 16)
                sp.wait_ge(s["sort_placed"], ROWS + 1)
                sp.dma_start(rec[0:ROWS, :], srt).then_inc(s["sort_back"], 16)
                sp.wait_ge(s["sort_back"], 16)
            sp.sem_inc(s["in_order"], 1)
            sp.dma_start(last_i[:], rec.rearrange("c e -> e c")[2 * P - 1:2 * P, :], allow_slow_non_contiguous=True).then_inc(s["s_lastd"], 16)
            sp.wait_ge(s["s_bias"], 32)
            early(0, EARLY1)
            sp.wait_ge(s["sch"], DLOC_DONE)
            sp.dma_start(dflat[:, 1:ROWT * P * P + 1].rearrange("o (k p e) -> (o p) k e", k=ROWT, e=P), erf[:, 3, :, :]).then_inc(s["s_dfl"], 16)
            sp.dma_start(dflat[:, 0:1], neg5[:, 0:1]).then_inc(s["s_dfl"], 16)
            sp.dma_start(dflat[:, ROWT * P * P + 1:ROWT * P * P + 2], neg5[:, 1:2]).then_inc(s["s_dfl"], 16)
            sp.wait_ge(s["s_dfl"], 48)
            sp.dma_start(shl[:, 0, :, :], dflat[:, 0:ROWT * P * P].rearrange("o (k p e) -> (o p) k e", k=ROWT, e=P)).then_inc(s["s_shl"], 16)
            sp.dma_start(shl[:, 1, :, :], dflat[:, 2:ROWT * P * P + 2].rearrange("o (k p e) -> (o p) k e", k=ROWT, e=P)).then_inc(s["s_shl"], 16)

            early(EARLY1, EARLY2)
            sp.wait_ge(s["sch"], SHIFT_DONE)
            sp.dma_start(pen_rows.rearrange("o (k p e) -> (o p) k e", k=ROWT, e=P), erf[:, 5, :, :]).then_inc(s["s_prow"], 16)

            early(EARLY2, EARLY3)
            early(EARLY3, TILES - 1)
            store_tile(TILES - 1, 0)

            def load_penalty(b, j):
                sp.dma_start(pen_s[:, j, :], pen_rows[:, bass.ds(B * P * b, B * P)].broadcast_to((RH, B * P))).then_inc(s["pen0"] if j == 0 else s["pen1"], 16)

            sp.wait_ge(s["s_prow"], 16)
            load_penalty(0, 0)
            load_penalty(1, 1)
            sp.dma_start(w_val[:].rearrange("k r (h d) -> k (r h) d", h=H), w_v.rearrange("r h k d -> k (r h) d")).then_inc(s["s_wv"], 16)
            sp.dma_start(wo_raw[:], out_w).then_inc(s["s_wo"], 16)
            for t, v in ((ob_all, out_b), (ga_all, gamma), (be_all, beta)):
                sp.dma_start(t[:], v.rearrange("(a c) -> a c", a=1).broadcast_to((P, HID))).then_inc(s["s_vecs"], 16)

            def next_penalty(b, j):
                sp.wait_ge(s["f_ready"], upto(b))
                sp.sem_inc(s["sp_turn"], 1)
                load_penalty(b + 2, j)

            def store_values(t, j):
                sp.wait_ge(s["v_out"], t + 1)
                sp.sem_inc(s["sp_turn"], 1)
                sp.dma_start(v_tab[bass.ds(t * (P * R), P * R), :].rearrange("(p r) c -> p r c", r=R),
                             vst[:, j, :].rearrange("p (r c) -> p r c", r=R)).then_inc(s["vst0"] if j == 0 else s["vst1"], 16)

            def penalty_and_values(b, j):
                next_penalty(b, j)
                store_values(b - 1, 1 - j)

            next_penalty(0, 0)
            penalty_and_values(1, 1)
            pairs(sp, 2, LAG, penalty_and_values)
            pairs(sp, LAG, NB - 2, next_penalty)
            sp.wait_ge(s["x_room"], 1)
            sp.dma_start(x_n[:, 0:TILES - 1, :], x_full).then_inc(s["s_x"], 16)
            sp.dma_start(x_n[0:LASTN, TILES - 1, :], x[(TILES - 1) * P:N, :]).then_inc(s["s_x"], 16)

            for g, tiles in enumerate(GROUPS):
                full = [t for t in tiles if t < TILES - 1]
                sp.wait_ge(s["fin"], g + 1)
                if full:
                    a, e = full[0], full[-1] + 1
                    sp.dma_start(out[a * P:e * P, :].rearrange("(t p) d -> p t d", p=P), sq[:, a:e, :]).then_inc(s["s_out"], 16)
            sp.dma_start(out[(TILES - 1) * P:N, :], sq[0:LASTN, TILES - 1, :]).then_inc(s["s_out"], 16)
            sp.wait_ge(s["s_out"], 16 * (len([g for g in GROUPS if g[0] < TILES - 1]) + 1))

        @block.gpsimd
        def _(pool):
            nc.gpsimd.memset(pad_row[:, 0:3 * P], 0).then_inc(s["s_ip"], 1)
            pool.wait_ge(s["s_ip"], 1)
            nc.gpsimd.memset(pad_row[:, P:2 * P], NPAD - 1).then_inc(s["s_pad"], 1)
            nc.gpsimd.memset(neg5[:], -5.0e5).then_inc(s["s_pad"], 1)
            nc.gpsimd.iota(iota_i[:], [[1, P]], base=0, channel_multiplier=0).then_inc(s["s_const"], 1)
            nc.gpsimd.iota(crow_i[:], [[1, RROWS]], base=0, channel_multiplier=0).then_inc(s["s_const"], 1)
            nc.gpsimd.iota(step_i[:], [[P, ROWT]], base=0, channel_multiplier=1).then_inc(s["s_const"], 1)
            nc.gpsimd.memset(zeros[:], 0.0)
            nc.gpsimd.memset(ones[:], 1.0).then_inc(s["s_const"], 1)
            nc.gpsimd.memset(ident[:], 0.0).then_inc(s["s_id"], 1)
            pool.wait_ge(s["s_id"], 1)
            nc.gpsimd.affine_select(out=ident[:], in_=ident[:], compare_op=ALU.not_equal, fill=1.0, base=0,
                                    pattern=[[-1, P]], channel_multiplier=1).then_inc(s["s_id"], 1)
            pool.wait_ge(s["flag_rdy"], 1)
            with pool.If(pool.value_load(unsorted_i[0:1, 0:1], min_val=0, max_val=1) > 0):
                pool.sem_inc(s["sort_placed"], 1)
                nc.gpsimd.affine_select(out=below, in_=ones[:], compare_op=ALU.is_gt, fill=0.0, base=0,
                                        pattern=[[-1, P]], channel_multiplier=1).then_inc(s["sort_mask"], 1)
                nc.gpsimd.affine_select(out=above, in_=ones[:], compare_op=ALU.is_gt, fill=0.0, base=0,
                                        pattern=[[1, P]], channel_multiplier=-1).then_inc(s["sort_mask"], 1)
                with pool.Fori(0, ROWS) as n:
                    pool.wait_ge(s["sort_spot"], n + 1)
                    pool.sem_inc(s["pool_turn"], 1)
                    for a in range(3):
                        nc.gpsimd.indirect_dma_start(srt.rearrange("c (w o) -> (c w) o", o=1), bass.IndirectOffsetOnAxis(ap=spot[:, a:a + 1], axis=0),
                                                     edge3[:, a:a + 1], None).then_inc(s["sort_out"], 16)
                    pool.wait_ge(s["sort_out"], 48 * n + 48)
                    pool.sem_inc(s["sort_placed"], 1)
            pool.wait_ge(s["in_order"], 1)
            pool.wait_ge(s["sch"], ROWI_DONE)
            for k in range(ROWT):
                nc.gpsimd.indirect_dma_start(erow[:, k, :, :].rearrange("p a e -> p (a e)"), None, rec,
                                             bass.IndirectOffsetOnAxis(ap=row_i[:, k:k + 1], axis=0)).then_inc(s["s_erow"], 16)
            pool.wait_ge(s["tab_out0"], 32 * (TILES - TILES // 2))
            pool.wait_ge(s["tab_out1"], 32 * (TILES // 2))
            with pool.Fori(0, NI) as i:
                for j in range(2):
                    b = 2 * i + j
                    pool.wait_ge(s["ist_ready"], upto(b))
                    pool.sem_inc(s["pool_turn"], 1)
                    done = s["kq0"] if j == 0 else s["kq1"]
                    for k in range(B):
                        nc.gpsimd.indirect_dma_start(kg[:, j, k, :], None, k_tab, bass.IndirectOffsetOnAxis(ap=ist[:, j, 0, k:k + 1], axis=0)).then_inc(done, 16)
                        nc.gpsimd.indirect_dma_start(qg[:, j, k, :], None, q_tab, bass.IndirectOffsetOnAxis(ap=ist[:, j, 1, k:k + 1], axis=0)).then_inc(done, 16)
            pool.wait_ge(s["vst0"], 16 * (TILES - TILES // 2))
            pool.wait_ge(s["vst1"], 16 * (TILES // 2))

            def gather_values(n, slot):
                pool.wait_ge(s["vist_ready"], upto(n))
                pool.sem_inc(s["pool_turn"], 1)
                for k in range(B):
                    nc.gpsimd.indirect_dma_start(vg[:, slot, k, :], None, v_tab,
                                                 bass.IndirectOffsetOnAxis(ap=ist[:, slot // 2, slot % 2, k:k + 1], axis=0)).then_inc(s[f"v{slot}"], 16)

            for q in range(4):
                gather_values(q, q)
            pool.wait_ge(s["i_ahead"], 1)
            for a in range(NB // 8):
                for k in range(B):
                    nc.gpsimd.indirect_dma_start(v_ahead[:, a, k, :], None, v_tab,
                                                 bass.IndirectOffsetOnAxis(ap=i_ahead[:, a, k:k + 1], axis=0)).then_inc(s["v_ahead"], 16)
            with pool.Fori(0, NB // 8 - 1) as i:
                for m, slot in enumerate(V_SLOT):
                    gather_values(7 * i + m + 4, slot)
            for slot in range(3):
                gather_values(7 * (NB // 8 - 1) + slot + 4, slot)

        @block.scalar
        def _(act):
            for name in ("ist_ready", "fe_ready", "c_oht", "c_p", "d_oh", "d_abs", "d_oht", "vist_ready"):
                act.sem_inc(s[name], CREDIT)
            for n, w in ((0, w_k), (1, w_q)):
                act.dma_start(w_kq[:, n, :, :].rearrange("k r (h d) -> k (r h) d", h=H), w.rearrange("r h k d -> k (r h) d")).then_inc(s["s_w"], 16)
            for j in range(2):
                act.dma_start(kqst[:, j, :, 0, HID:KW], attn_bias.rearrange("(a r) h -> a r h", a=1).broadcast_to((P, R, H))).then_inc(s["s_bias"], 16)

            def transposed_in(t, j):
                act.wait_ge(s["xt_ps"], t + 1)
                act.sem_inc(s["act_turn"], 1)
                nc.scalar.copy(xt_all[:, bass.ds(t, 1), :].rearrange("p o c -> p (o c)"), bank[2][:, 0:P])
                nc.scalar.copy(xt[:, j, :], bank[2][:, 0:P]).then_inc(s["xt_sb"], 1)

            def tables_out(t, j, free):
                if free is not None:
                    act.wait_ge(*free)
                for r in range(R):
                    act.wait_ge(s["tab_mm"], R * t + r + 1)
                    nc.scalar.mul(kqst[:, j, r, :, 0:HID], bank[3 + r][:, 0:2 * HID].rearrange("p (a c) -> p a c", a=2), KQ_SCALE).then_inc(s["tab_act"], 1)

            def load_after(t, j):
                act.dma_start(xs[:, j, :], x[bass.ds(t * P + 2 * P, P), :]).then_inc(s["s_xs0"] if j == 0 else s["s_xs1"], 16)

            transposed_in(0, 0)
            for t in range(2):
                load_after(t, t)
                transposed_in(t + 1, 1 - t)
                tables_out(t, t, None)
            with act.Fori(1, TILES // 2 - 1) as i:
                for j in range(2):
                    load_after(2 * i + j, j)
                    transposed_in(2 * i + j + 1, 1 - j)
                    tables_out(2 * i + j, j, (s["tab_out0"] if j == 0 else s["tab_out1"], 32 * i))
            act.dma_start(xs[0:LASTN, 0, :], x[(TILES - 1) * P:N, :]).then_inc(s["s_xs0"], 16)
            for j in range(2):
                transposed_in(TILES - 2 + j, 1 - j)
                tables_out(TILES - 3 + j, j, (s["tab_out0"] if j == 0 else s["tab_out1"], 32 * (TILES // 2 - 1)))
            tables_out(TILES - 1, 0, (s["tab_out0"], 32 * (TILES // 2)))

            act.wait_ge(s["edges_rdy"], 1)

            def stage_indices(b, j):
                nc.scalar.copy(ist[:, j, 0, :], kidx[:, bass.ds(B * b, B)])
                nc.scalar.copy(ist[:, j, 1, :], qidx[:, bass.ds(B * b, B)]).then_inc(s["ist_ready"], 1)

            stage_indices(0, 0)
            stage_indices(1, 1)

            def logits_batch(b, j):
                act.wait_ge(s["logit_done"], upto(b))
                act.sem_inc(s["act_turn"], 1)
                stage_indices(b + 2, j)

            def last_edges(b, j):
                act.wait_ge(s["tmax_mm"], upto(b - 2))
                act.wait_ge(s["fb_ready"], upto(b))
                act.sem_inc(s["act_turn"], 1)
                for k in range(B):
                    last = nc.scalar.activation(fe[:, j, k, :], back_ps[:, (j * B + k) * RH:(j * B + k + 1) * RH], ACT.Copy,
                                                scale=islast[:, bass.ds(B * b + k, 1)])
                last.then_inc(s["fe_ready"], 1)

            def one_hot_back(b, j):
                act.wait_ge(s["c_ex"], upto(b - 2))
                act.wait_ge(s["c_ohtp"], upto(b))
                nc.scalar.copy(oht[:, j, :, :].rearrange("p b n -> p (b n)"), turn_ps[j]).then_inc(s["c_oht"], 1)

            def exponential(b, j):
                act.wait_ge(s["c_z"], upto(b))
                act.sem_inc(s["act_turn"], 1)
                nc.scalar.activation(prob[:, bass.ds(B * b, B), :], zed[:, j, :, :], ACT.Exp).then_inc(s["c_p"], 1)

            def value_in(t, j):
                nc.scalar.copy(xt[:, j, :], xt_all[:, bass.ds(t, 1), :].rearrange("p o c -> p (o c)")).then_inc(s["v_in"], 1)

            def value_out(t, j, free):
                if free is not None:
                    act.wait_ge(*free)
                    act.sem_inc(s["act_turn"], 1)
                act.wait_ge(s["v_mul"], t + 1)
                nc.scalar.copy(vst[:, j, :], v_ps[j]).then_inc(s["v_out"], 1)

            def logits_and_values(b, j, first=False):
                logits_only(b, j)
                value_out(b - 1, 1 - j, None if first else (s["vst1"] if j == 0 else s["vst0"], 8 * (b - 2 + j)))
                value_in(b, j)

            def both_batches(b, j):
                logits_batch(b, j)
                exponential(b - LAG, j)
                one_hot_back(b - LAG + 1, 1 - j)
                last_edges(b, j)

            def logits_only(b, j):
                logits_batch(b, j)
                last_edges(b, j)

            def softmax_only(b, j):
                one_hot_back(b + 1, 1 - j)
                exponential(b, j)

            act.wait_ge(s["xt_sb"], TILES)
            logits_only(0, 0)
            value_in(0, 0)
            logits_and_values(1, 1, True)
            logits_and_values(2, 0, True)
            logits_and_values(3, 1)
            with act.Fori(2, LAG // 2 - 1) as i:
                for j in range(2):
                    logits_and_values(2 * i + j, j)
            logits_and_values(LAG - 2, 0)
            logits_only(LAG - 1, 1)
            value_out(TILES - 1, 0, (s["vst0"], 16 * ((TILES - 1) // 2)))
            act.wait_ge(s["long_rdy"], 1)
            with act.If(short_of(act) > 0):
                one_hot_back(0, 0)
                pairs(act, LAG, NB, both_batches)
            with act.If(long_of(act) > 0):
                pairs(act, LAG, NB, logits_only)
                one_hot_back(0, 0)
                pairs(act, 0, NB - LAG, softmax_only)

            def stage_value_indices(b, q):
                nc.scalar.copy(ist[:, q // 2, q % 2, :], kidx[:, bass.ds(B * b, B)]).then_inc(s["vist_ready"], 1)

            act.wait_ge(s["ist_ready"], upto(NB + 1))
            for q in range(4):
                stage_value_indices(q, q)
            nc.scalar.copy(i_ahead[:], kidx[:, 0:STEPS].rearrange("p (a c) -> p a c", c=8 * B)[:, :, 7 * B:]).then_inc(s["i_ahead"], 1)
            fours(act, lambda b, q: softmax_only(b, q % 2))
            softmax_only(NB - 2, 0)
            exponential(NB - 1, 1)
            act.wait_ge(s["nd_rdy"], 1)

            def one_hots(b, slot):
                act.wait_ge(s["v_mm"], upto(b - 4))
                act.sem_inc(s["act_turn"], 1)
                for k in range(B):
                    last = nc.scalar.activation(oh[:, slot, k, :], iota_n[:], ACT.Abs, bias=neg_dloc[:, bass.ds(B * b + k, 1)])
                last.then_inc(s["d_abs"], 1)
                flat = oh[:, slot, :, :].rearrange("p b n -> p (b n)")
                act.wait_ge(s["d_abs"], upto(b))
                nc.scalar.activation(flat, flat, ACT.Relu, scale=-1.0, bias=1.0).then_inc(s["d_oh"], 1)

            one_hots(0, 0)
            one_hots(1, 1)
            with act.Fori(0, NB // 8) as i:
                for q in range(8):
                    b = 8 * i + q
                    act.wait_ge(s["d_ex"], upto(b - 2))
                    act.wait_ge(s["d_ohtp"], upto(b))
                    nc.scalar.copy(oht_v[:, q % 2, :, :].rearrange("p b n -> p (b n)"), bank[7]).then_inc(s["d_oht"], 1)
                    if q >= 1:
                        act.wait_ge(s["wv_ready"], upto(b - 1))
                        act.sem_inc(s["act_turn"], 1)
                        stage_value_indices(b + (7 if q == 4 else 3), V_SLOT[q - 1])
                    one_hots(b + 2, (q + 2) % 4)
            act.wait_ge(s["s_wot"], 1)
            nc.scalar.copy(wo_t[:], bank[7][:, 0:P]).then_inc(s["wo_in"], 1)
            act.wait_ge(s["v_mm"], upto(NB - 1))
            nc.scalar.copy(agg[:].rearrange("p t c -> p (t c)")[:, 512 * HALF_G:], agg_ps[:, 512 * HALF_G:]).then_inc(s["agg_act"], 1)

            def sums_of_squares(n, g, values):
                act.wait_ge(s["mu_rdy"], n * len(GROUPS) + g + 1)
                for k, t in enumerate(GROUPS[g]):
                    last = nc.scalar.activation(sq[:, t, :], values(g, k, t), ACT.Square, bias=neg_mu[:, n, t:t + 1], accum_out=rstd[:, n, t:t + 1])
                last.then_inc(s["var_rdy"], 1)

            def projected(g, k, t):
                return bank[g][:, k * P:(k + 1) * P]

            for g, tiles in enumerate(GROUPS):
                act.wait_ge(s["o_tr"], g + 1)
                if g >= 2:
                    act.wait_ge(s["o_mm"], g - 1)
                nc.scalar.copy(agt[:, g % 2, 0:len(tiles), :].rearrange("p b n -> p (b n)"), bank[7][:, 0:P * len(tiles)]).then_inc(s["o_cp"], 1)
                if g >= 1:
                    sums_of_squares(0, g - 1, projected)
            sums_of_squares(0, len(GROUPS) - 1, projected)
            act.wait_ge(s["sq_ask"], 1)
            nc.scalar.activation(rstd[:, 0, :], rstd[:, 0, :], ACT.Sqrt).then_inc(s["sq_got"], 1)
            for g in range(len(GROUPS)):
                sums_of_squares(1, g, lambda g, k, t: hh[:, t, :])
            act.wait_ge(s["sq_ask"], 2)
            nc.scalar.activation(rstd[:, 1, :], rstd[:, 1, :], ACT.Sqrt).then_inc(s["sq_got"], 1)

        @block.tensor
        def _(pe):
            mm = nc.tensor.matmul
            for name in ("mlt_ready", "fb_ready", "tmax_mm", "c_ohtp", "c_ex", "c_den", "d_ohtp", "d_ex", "v_mm"):
                pe.sem_inc(s[name], CREDIT)

            def addrs_of(which, b):
                return nc.values_load_multi_w_load_instructions(
                    addr_row[0:1, which, bass.ds(B * b, B)], engines=[mybir.EngineType.PE], min_val=0,
                    max_val=(TILES - 1) * (P if which else RH), skip_runtime_bounds_check_because="tiles are clamped to TILES - 1 when the schedule is made")[1]

            def window_addrs_of(b):
                return nc.values_load_multi_w_load_instructions(
                    rel_row[0:1, bass.ds(B * b, B)], engines=[mybir.EngineType.PE], min_val=0, max_val=WIN - RH,
                    skip_runtime_bounds_check_because="a step is at most one node tile on from the step before")[1]

            pe.wait_ge(s["s_id"], 2)
            pe.wait_ge(s["s_const"], 4)
            pe.wait_ge(s["chk_done"], 2)
            mm(bank[0][0:1, 0:1], fell[0:CHK_P, :], ones[0:CHK_P, 0:1], start=True, stop=True).then_inc(s["fell_ps"], 1)
            pe.wait_ge(s["flag_rdy"], 1)
            with pe.If(pe.value_load(unsorted_i[0:1, 0:1], min_val=0, max_val=1) > 0):
                with pe.Fori(0, ROWS) as n:
                    pe.wait_ge(s["sort_oh"], n + 1)
                    pe.sem_inc(s["pe_turn"], 1)
                    mm(bank[1][:, 0:TILES], oh_lo, oh_hi, start=True, stop=True).then_inc(s["sort_cnt"], 1)
                pe.wait_ge(s["sort_base"], 1)
                pe.wait_ge(s["sort_mask"], 2)
                mm(bank[2][:, 0:TILES], ones[:], prefix, start=True, stop=False)
                mm(bank[2][:, 0:TILES], above, count, start=False, stop=True).then_inc(s["sort_start"], 1)
                with pe.Fori(0, ROWS) as n:
                    pe.wait_ge(s["sort_oh"], n + ROWS + 1)
                    pe.sem_inc(s["pe_turn"], 1)
                    mm(bank[1][:, 0:TILES], oh_lo, oh_hi, start=True, stop=True).then_inc(s["sort_cnt"], 1)
                    nc.tensor.transpose(bank[3][:, 0:P], oh_lo, ident[:])
                    nc.tensor.transpose(bank[3][:, P:2 * P], dst_rep, ident[:]).then_inc(s["sort_t"], 1)
                    pe.wait_ge(s["sort_tc"], n + 1)
                    pe.sem_inc(s["pe_turn"], 1)
                    mm(bank[2][:, 0:TILES], oh_lo_t, start, start=True, stop=True).then_inc(s["sort_rk"], 1)
                pe.wait_ge(s["sort_add"], 2 * ROWS + 1)

            def transpose_tile(t, j, loads):
                pe.wait_ge(s["s_xs0"] if j == 0 else s["s_xs1"], loads)
                nc.tensor.transpose(bank[2][:, 0:P], xs[:, j, :], ident[:]).then_inc(s["xt_ps"], 1)

            def multiply_tile(t, j, first=False):
                for r in range(R):
                    if not first:
                        pe.wait_ge(s["tab_act"], R * t - R + r + 1)
                    mm(bank[3 + r][:, 0:2 * HID], xt[:, j, :], w_kq[:, :, r, :],
                       start=True, stop=True).then_inc(s["tab_mm"], 1)

            def table_tile(t, j, loads, first=False):
                pe.wait_ge(s["xt_sb"], t + 1)
                transpose_tile(t + 1, 1 - j, loads)
                multiply_tile(t, j, first)

            def early(first, end):
                with pe.Fori(first // 2, end // 2) as i:
                    for j in range(2):
                        table_tile(2 * i + j, j, 16 * (i + 1 + j))

            transpose_tile(0, 0, 16)
            pe.wait_ge(s["s_w"], 32)
            table_tile(0, 0, 16, True)
            table_tile(1, 1, 32)
            pe.wait_ge(s["sch"], CPLUS_DONE)
            mm(bank[0][:, 0:RROWS], ones[0:1, :], cplus[:], start=True, stop=True).then_inc(s["sch_ps"], 1)

            early(EARLY0, EARLY1)
            pe.wait_ge(s["sch"], ADDR_DONE)
            for n in range(2):
                for k in range(ROWT):
                    last = mm(bank[1 - n][0:1, k * P:(k + 1) * P], addr2[:, k, n:n + 1], ident[:], start=True, stop=True)
            last.then_inc(s["addr_ps"], 1)
            for n in range(5):
                if n == 0:
                    early(EARLY1, EARLY2)
                    pe.wait_ge(s["sch"], DLOC_DONE)
                if n == 4:
                    early(EARLY2, EARLY3)
                    pe.wait_ge(s["sch"], SHIFT_DONE)
                if n >= 2:
                    pe.wait_ge(s["tr_sb"], n - 1)
                for k in range(ROWT):
                    last = nc.tensor.transpose(bank[n % 2][:, k * P:(k + 1) * P], erf[:, n, k, :], ident[:])
                last.then_inc(s["tr_ps"], 1)

            early(EARLY3, TILES - 1)
            pe.wait_ge(s["xt_sb"], TILES)
            multiply_tile(TILES - 1, 0)
            pe.wait_ge(s["s_wv"], 16)
            pe.wait_ge(s["zero_rdy"], 1)

            def masked_logits(b, j):
                pe.wait_ge(s["f_ready"], upto(b - 2))
                pe.wait_ge(s["ml_ready"], upto(b))
                pe.sem_inc(s["pe_turn"], 1)
                for k in range(B):
                    last = nc.tensor.transpose(ml_ps[j][0:RH, k * P:(k + 1) * P], ml[:, j, k, :, :].rearrange("p r h -> p (r h)"), ident[:])
                last.then_inc(s["mlt_ready"], 1)

            def maxima_back(b, j):
                pe.wait_ge(s["fe_ready"], upto(b - 2))
                pe.wait_ge(s["f_ready"], upto(b))
                pe.sem_inc(s["pe_turn"], 1)
                for k in range(B):
                    last = nc.tensor.transpose(back_ps[:, (j * B + k) * RH:(j * B + k + 1) * RH], fwd[:, j, k * P:(k + 1) * P], ident[0:RH, 0:RH])
                last.then_inc(s["fb_ready"], 1)

            def to_nodes(window, at, one_hot, values, done):
                mm(window, zeros[0:1, 0:P], zeros[0:1, :], start=True, stop=True)
                for k in range(B):
                    last = mm(window[:, bass.ds(at[k], RH)], one_hot[:, k, :], values[:, k, :],
                              start=False, stop=True, skip_group_check=True)
                last.then_inc(done, 1)

            def maxima_to_nodes(b, j):
                at = window_addrs_of(b)
                pe.wait_ge(s["oh_ready"], upto(b))
                pe.wait_ge(s["t_acc"], upto(b))
                pe.wait_ge(s["fe_ready"], upto(b))
                pe.sem_inc(s["pe_turn"], 1)
                to_nodes(win_t, at, oh[:, j, :, :], fe[:, j, :, :], s["tmax_mm"])

            def sums_to_nodes(b, j, slot):
                at = window_addrs_of(b)
                pe.wait_ge(s["d_acc"], upto(b))
                pe.wait_ge(s["c_pm"], upto(b))
                pe.sem_inc(s["pe_turn"], 1)
                to_nodes(win_d, at, oh[:, slot, :, :], pm[:, j, :, :, :].rearrange("p b r h -> p b (r h)"), s["c_den"])

            def turn_c(b, j, slot):
                pe.wait_ge(s["c_oht"], upto(b - 2))
                pe.wait_ge(s["c_oh"], upto(b))
                for k in range(B):
                    last = nc.tensor.transpose(turn_ps[j][:, k * P:(k + 1) * P], oh[:, slot, k, :], ident[:])
                last.then_inc(s["c_ohtp"], 1)

            def expand_c(b, j, maxima):
                at = addrs_of(0, b)
                pe.wait_ge(s["c_sel"], upto(b - 1))
                pe.wait_ge(s["c_oht"], upto(b))
                pe.wait_ge(s["t_acc"], upto(maxima + 1))
                pe.sem_inc(s["pe_turn"], 1)
                for k in range(B):
                    last = mm(exp_ps[:, k * RH:(k + 1) * RH], oht[:, j, k, :], node_max[:, bass.ds(at[k], RH)], start=True, stop=True)
                last.then_inc(s["c_ex"], 1)

            def both_batches(b, j, first=False):
                masked_logits(b, j)
                if not first:
                    sums_to_nodes(b - LAG - 1, 1 - j, 3 - j)
                maxima_to_nodes(b - 1, 1 - j)
                turn_c(b - LAG + 1, 1 - j, 3 - j)
                maxima_back(b, j)
                expand_c(b - LAG + 1, 1 - j, b - 2)

            def multiply_values(t, j, first):
                if not first:
                    pe.wait_ge(s["v_out"], t - 1)
                    pe.sem_inc(s["pe_turn"], 1)
                pe.wait_ge(s["v_in"], t + 1)
                mm(v_ps[j][:, 0:512], xt[:, j, :], w_flat[:, 0:512], start=True, stop=True)
                mm(v_ps[j][:, 512:R * HID], xt[:, j, :], w_flat[:, 512:R * HID], start=True, stop=True).then_inc(s["v_mul"], 1)

            w_flat = w_val[:].rearrange("p r c -> p (r c)")

            def logits_only(b, j, first=False):
                masked_logits(b, j)
                if not first:
                    maxima_to_nodes(b - 1, 1 - j)
                maxima_back(b, j)

            def logits_and_values(b, j, first=False):
                masked_logits(b, j)
                maxima_to_nodes(b - 1, 1 - j)
                multiply_values(b - 1, 1 - j, first)
                maxima_back(b, j)

            def softmax_only(b, j, first=False):
                if not first:
                    sums_to_nodes(b - 1, 1 - j, 3 - j)
                turn_c(b + 1, 1 - j, 3 - j)
                expand_c(b + 1, 1 - j, NB - 1)

            logits_only(0, 0, True)
            logits_and_values(1, 1, True)
            logits_and_values(2, 0, True)
            logits_and_values(3, 1)
            pairs(pe, 4, LAG, logits_and_values)
            pe.wait_ge(s["v_out"], TILES)
            pe.wait_ge(s["long_rdy"], 1)
            with pe.If(short_of(pe) > 0):
                turn_c(0, 0, 2)
                expand_c(0, 0, LAG - 3)
                both_batches(LAG, 0, True)
                both_batches(LAG + 1, 1)
                pairs(pe, LAG + 2, NB, both_batches)
                maxima_to_nodes(NB - 1, 1)
            with pe.If(long_of(pe) > 0):
                pairs(pe, LAG, NB, logits_only)
                maxima_to_nodes(NB - 1, 1)
                turn_c(0, 0, 2)
                expand_c(0, 0, NB - 1)
                softmax_only(0, 0, True)
                softmax_only(1, 1)
                pairs(pe, 2, NB - LAG, softmax_only)

            def softmax_end(b, q, before):
                turn_c(b + 1, 1 - q % 2, end_slot(q + 1))
                sums_to_nodes(b - 1, 1 - q % 2, before)
                expand_c(b + 1, 1 - q % 2, NB - 1)

            fours(pe, lambda b, q: softmax_end(b, q, end_slot(q + 3)))
            softmax_end(NB - 2, 0, end_slot(3))
            sums_to_nodes(NB - 2, 0, end_slot(0))
            sums_to_nodes(NB - 1, 1, end_slot(1))

            pe.wait_ge(s["nden_rdy"], 1)

            def turn_d(b, q):
                pe.wait_ge(s["d_sel"], upto(b - 1))
                pe.wait_ge(s["d_oh"], upto(b))
                for k in range(B):
                    last = nc.tensor.transpose(bank[7][:, k * P:(k + 1) * P], oh[:, q, k, :], ident[:])
                last.then_inc(s["d_ohtp"], 1)

            def expand_d(b, q):
                at = addrs_of(0, b)
                pe.wait_ge(s["d_oht"], upto(b))
                pe.sem_inc(s["pe_turn"], 1)
                for k in range(B):
                    last = mm(bank[7][:, 3 * k * RH:3 * (k + 1) * RH], oht_v[:, q % 2, k, :],
                              node3[:].rearrange("p g n h -> p (g n h)")[:, bass.ds(at[k] * 3, 3 * RH)], start=True, stop=True)
                last.then_inc(s["d_ex"], 1)

            def aggregate(b, q):
                at = addrs_of(1, b)
                pe.wait_ge(s["wv_ready"], upto(b))
                pe.sem_inc(s["pe_turn"], 1)
                for k in range(B):
                    last = mm(agg_ps[:, bass.ds(at[k], HID)], oh[:, q, k, :], prod[:, q % 2, k, :],
                              start=False, stop=True, skip_group_check=True)
                last.then_inc(s["v_mm"], 1)

            turn_d(0, 0)
            expand_d(0, 0)
            turn_d(1, 1)
            expand_d(1, 1)
            with pe.Fori(0, NB // 4 - 1) as i:
                for q in range(4):
                    turn_d(4 * i + q + 2, (q + 2) % 4)
                    aggregate(4 * i + q, q)
                    expand_d(4 * i + q + 2, (q + 2) % 4)
            for b in range(NB - 4, NB - 2):
                turn_d(b + 2, (b + 2) % 4)
                aggregate(b, b % 4)
                expand_d(b + 2, (b + 2) % 4)
            aggregate(NB - 2, 2)
            aggregate(NB - 1, 3)

            pe.wait_ge(s["s_wo"], 16)
            nc.tensor.transpose(bank[7][:, 0:P], wo_raw[:], ident[:]).then_inc(s["s_wot"], 1)

            def turn_group(g):
                if g >= 1:
                    pe.wait_ge(s["o_cp"], g)
                for k, t in enumerate(GROUPS[g]):
                    last = nc.tensor.transpose(bank[7][:, k * P:(k + 1) * P], agg[:, t, :], ident[:])
                last.then_inc(s["o_tr"], 1)

            def project(g):
                pe.wait_ge(s["o_cp"], g + 1)
                for k, t in enumerate(GROUPS[g]):
                    to = bank[g][:, k * P:(k + 1) * P]
                    mm(to, ident[:], x_n[:, t, :], start=True, stop=False)
                    last = mm(to, agt[:, g % 2, k, :], wo_t[:], start=False, stop=True)
                last.then_inc(s["o_mm"], 1)

            pe.wait_ge(s["wo_in"], 1)
            pe.wait_ge(s["agg_rdy"], 1)
            pe.wait_ge(s["agg_act"], 1)
            pe.wait_ge(s["x_sums"], TILES)
            turn_group(0)
            for g in range(1, len(GROUPS)):
                turn_group(g)
                project(g - 1)
            project(len(GROUPS) - 1)

        @block.vector
        def _(dve):
            V = nc.vector
            for name in ("logit_done", "ml_ready", "oh_ready", "f_ready", "t_acc", "d_acc", "c_oh", "c_sel", "c_z", "c_pm", "d_sel", "wv_ready"):
                dve.sem_inc(s[name], CREDIT)

            class Chain:

                def __init__(self, name, base=0):
                    self.sem, self.n, self.base = s[name], 0, base

                def link(self, ins):
                    self.n += 1
                    ins.then_inc(self.sem, 1)
                    dve.wait_ge(self.sem, self.base + self.n)

            dve.wait_ge(s["s_chk"], 48)
            V.tensor_tensor(falls, chk[:, 0:CHK_C], chk[:, 1:CHK_C + 1], ALU.is_gt).then_inc(s["chk_done"], 1)
            dve.wait_ge(s["chk_done"], 1)
            V.tensor_reduce(fell[0:CHK_P, :], falls, AX_X, ALU.max).then_inc(s["chk_done"], 1)
            dve.wait_ge(s["fell_ps"], 1)
            V.tensor_scalar(unsorted_i[:], bank[0][0:1, 0:1], 1.0, None, ALU.min).then_inc(s["flag_rdy"], 1)
            dve.wait_ge(s["s_const"], 4)
            dve.wait_ge(s["flag_rdy"], 1)
            with dve.If(dve.value_load(unsorted_i[0:1, 0:1], min_val=0, max_val=1) > 0):
                SPLIT = 7

                def split_edge(c, row):
                    dve.wait_ge(s["sort_in"], 16 * row + 16)
                    c.link(V.tensor_copy(dst_f, edge3[:, 1:2]))
                    c.link(V.tensor_scalar(hi_i, edge3[:, 1:2], 7, None, ALU.logical_shift_right))
                    c.link(V.tensor_copy(hi_f, hi_i))
                    c.link(V.tensor_scalar(lo_f, hi_f, -float(P), None, ALU.mult))
                    c.link(V.tensor_tensor(lo_f, lo_f, dst_f, ALU.add))
                    c.link(V.tensor_scalar(oh_lo, iota_n[:], lo_f, None, ALU.is_equal))
                    c.link(V.tensor_scalar(oh_hi, iota_n[:, 0:TILES], hi_f, None, ALU.is_equal))

                V.tensor_copy(iota_n[:], iota_i[:]).then_inc(s["sort_zero"], 1)
                V.memset(count, 0.0).then_inc(s["sort_zero"], 1)
                dve.wait_ge(s["sort_zero"], 2)
                dve.sem_inc(s["sort_add"], 1)
                with dve.Fori(0, ROWS) as n:
                    c = Chain("sort_dve", SPLIT * n)
                    split_edge(c, n)
                    assert c.n == SPLIT
                    dve.sem_inc(s["sort_oh"], 1)
                    dve.wait_ge(s["sort_cnt"], n + 1)
                    V.tensor_tensor(count, count, bank[1][:, 0:TILES], ALU.add).then_inc(s["sort_add"], 1)
                dve.wait_ge(s["sort_add"], ROWS + 1)
                V.memset(prefix[:, 0:1], 0.0).then_inc(s["sort_zero"], 1)
                for t in range(1, TILES):
                    dve.wait_ge(s["sort_zero"], t + 2)
                    V.tensor_tensor(prefix[:, t:t + 1], prefix[:, t - 1:t], count[:, t - 1:t], ALU.add).then_inc(s["sort_zero"], 1)
                dve.wait_ge(s["sort_zero"], TILES + 2)
                dve.sem_inc(s["sort_base"], 1)
                dve.wait_ge(s["sort_start"], 1)
                V.tensor_copy(start, bank[2][:, 0:TILES]).then_inc(s["sort_zero"], 1)
                dve.wait_ge(s["sort_zero"], TILES + 3)
                PLACE = SPLIT + 13
                with dve.Fori(0, ROWS) as n:
                    c = Chain("sort_dve", PLACE * n + SPLIT * ROWS)
                    split_edge(c, n + ROWS)
                    V.tensor_scalar(dst_rep, ones[:], dst_f, None, ALU.mult).then_inc(s["sort_oh"], 1)
                    dve.wait_ge(s["sort_t"], n + 1)
                    V.tensor_copy(oh_lo_t, bank[3][:, 0:P]).then_inc(s["sort_tc"], 1)
                    c.link(V.tensor_scalar(same, bank[3][:, P:2 * P], dst_f, None, ALU.is_equal))
                    c.link(V.tensor_tensor(same, same, below, ALU.mult))
                    c.link(V.tensor_reduce(before, same, AX_X, ALU.add))
                    dve.wait_ge(s["sort_rk"], n + 1)
                    c.link(V.tensor_tensor(here, bank[2][:, 0:TILES], oh_hi, ALU.mult))
                    c.link(V.tensor_reduce(rank, here, AX_X, ALU.add))
                    c.link(V.tensor_tensor(rank, rank, before, ALU.add))
                    c.link(V.tensor_copy(rank_i, rank))
                    c.link(V.tensor_scalar(hi_i, rank_i, 7, None, ALU.logical_shift_right))
                    c.link(V.tensor_scalar(spot_f, hi_i, float(2 * P), None, ALU.mult))
                    c.link(V.tensor_tensor(spot_f, spot_f, rank, ALU.add))
                    c.link(V.tensor_copy(spot[:, 0:1], spot_f))
                    c.link(V.tensor_scalar(spot[:, 1:2], spot_f, float(P), None, ALU.add))
                    c.link(V.tensor_scalar(spot[:, 2:3], spot_f, float(2 * P), None, ALU.add))
                    assert c.n == PLACE
                    dve.sem_inc(s["sort_spot"], 1)
                    V.tensor_tensor(start, start, bank[1][:, 0:TILES], ALU.add).then_inc(s["sort_add"], 1)

            sch = Chain("sch")
            dve.wait_ge(s["s_lastd"], 16)
            sch.link(V.tensor_scalar(tile_i[:], last_i[:], 7, None, ALU.logical_shift_right))
            sch.link(V.tensor_copy(crow[:], crow_i[:]))
            sch.link(V.tensor_tensor(cplus[:], tile_i[:], crow[:], ALU.add))
            assert sch.n == CPLUS_DONE
            sch.link(V.tensor_copy(step_id[:], step_i[:]))
            sch.link(V.tensor_copy(iota_n[:], iota_i[:]))
            dve.wait_ge(s["sch_ps"], 1)
            for k in range(ROWT):
                V.tensor_scalar(less[:, k, :], bank[0][:, 0:RROWS], step_id[:, k:k + 1], None, ALU.is_lt).then_inc(s["dve_turn"], 1)
            dve.wait_ge(s["dve_turn"], ROWT)
            sch.link(V.tensor_reduce(row_f[:], less[:], AX_X, ALU.add))
            sch.link(V.tensor_scalar(row_f[:], row_f[:], float(ROWS), None, ALU.min))
            sch.link(V.tensor_copy(row_i[:], row_f[:]))
            assert sch.n == ROWI_DONE
            sch.link(V.tensor_tensor(tile_f[:], step_id[:], row_f[:], ALU.subtract))
            sch.link(V.tensor_scalar(tile_f[:], tile_f[:], float(TILES - 1), None, ALU.min))
            sch.link(V.tensor_scalar(addr2[:, :, 0], tile_f[:], float(RH), None, ALU.mult))
            sch.link(V.tensor_scalar(addr2[:, :, 1], tile_f[:], float(P), None, ALU.mult))
            assert sch.n == ADDR_DONE
            dve.wait_ge(s["addr_ps"], 1)
            V.tensor_copy(addr_row[:, 0, :], bank[1][0:1, :]).then_inc(s["addr_rdy"], 1)
            V.tensor_copy(addr_row[:, 1, :], bank[0][0:1, :]).then_inc(s["addr_rdy"], 1)
            dve.wait_ge(s["addr_rdy"], 2)
            by_batch = addr_row[:, 0, 0:STEPS].rearrange("o (b k) -> o b k", k=B)
            V.tensor_tensor(rel_row[:].rearrange("o (b k) -> o b k", k=B), by_batch, by_batch[:, :, 0:1].broadcast_to((1, NB, B)), ALU.subtract).then_inc(s["addr_rdy"], 1)
            V.memset(acc_row[:, 0:1], 0).then_inc(s["addr_rdy"], 1)
            V.tensor_copy(acc_row[:, 1:NB + 1], by_batch[:, :, 0]).then_inc(s["addr_rdy"], 1)
            V.tensor_tensor(spans[:], addr_row[:, 0, 0:STEPS - SPAN - 1], addr_row[:, 0, SPAN + 1:STEPS], ALU.is_equal).then_inc(s["addr_rdy"], 1)
            dve.wait_ge(s["addr_rdy"], 6)
            V.tensor_reduce(fell[0:1, :], spans[:], AX_X, ALU.max).then_inc(s["addr_rdy"], 1)
            dve.wait_ge(s["addr_rdy"], 7)
            V.tensor_copy(long_i[:, 0:1], fell[0:1, :])
            V.tensor_scalar(long_i[:, 1:2], fell[0:1, :], 0.0, None, ALU.is_equal).then_inc(s["long_rdy"], 1)
            dve.wait_ge(s["s_erow"], 16 * ROWT)
            sch.link(V.tensor_copy(esf[:], erow[:]))
            sch.link(V.tensor_scalar(erf[:, 0, :, :], esf[:, :, 0, :], float(R), None, ALU.mult))
            sch.link(V.tensor_tensor(erf[:, 0, :, :], erf[:, 0, :, :], esf[:, :, 2, :], ALU.add))
            sch.link(V.tensor_scalar(erf[:, 1, :, :], esf[:, :, 1, :], float(R), None, ALU.mult))
            sch.link(V.tensor_tensor(erf[:, 1, :, :], erf[:, 1, :, :], esf[:, :, 2, :], ALU.add))
            sch.link(V.tensor_copy(erf[:, 2, :, :], esf[:, :, 2, :]))
            sch.link(V.tensor_tensor(erf[:, 3, :, :], esf[:, :, 1, :], addr2[:, :, 1:2].broadcast_to((P, ROWT, P)), ALU.subtract))
            assert sch.n == DLOC_DONE
            dve.wait_ge(s["s_shl"], 32)
            sch.link(V.tensor_tensor(erf[:, 4, :, :], erf[:, 3, :, :], shl[:, 1, :, :], ALU.not_equal))
            sch.link(V.tensor_tensor(erf[:, 5, :, :], erf[:, 3, :, :], shl[:, 0, :, :], ALU.not_equal))
            sch.link(V.tensor_scalar(erf[:, 5, :, :], erf[:, 5, :, :], -BIG, None, ALU.mult))
            assert sch.n == SHIFT_DONE
            for n, t in enumerate((kidx, qidx, ety, dloc, islast)):
                dve.wait_ge(s["tr_ps"], n + 1)
                V.tensor_copy(t[:], bank[n % 2]).then_inc(s["tr_sb"], 1)
            dve.wait_ge(s["tr_sb"], 5)
            for r in range(R):
                V.tensor_scalar(tmask[:, :, r], ety[:, 0:STEPS], float(r), None, ALU.is_equal).then_inc(s["dve_turn"], 1)
            dve.wait_ge(s["dve_turn"], ROWT + R)
            V.tensor_scalar(tpen[:], tmask[:], 1.0, BIG, ALU.subtract, ALU.mult).then_inc(s["edges_rdy"], 1)
            V.memset(fwd[:, 1, B * P - 1:B * P], -BIG).then_inc(s["dve_turn"], 1)

            V.memset(node_max[:], 0.0).then_inc(s["win_zero"], 1)
            V.memset(node_sum[:], 0.0).then_inc(s["win_zero"], 1)
            dve.wait_ge(s["tab_act"], R * TILES)
            V.memset(win_t, 0.0).then_inc(s["zero_rdy"], 1)
            dve.wait_ge(s["win_zero"], 2)
            dve.wait_ge(s["zero_rdy"], 1)

            def one_hots(b, slot, done):
                for k in range(B):
                    last = V.tensor_scalar(oh[:, slot, k, :], iota_n[:], dloc[:, bass.ds(B * b + k, 1)], None, ALU.is_equal)
                last.then_inc(done, 1)

            def per_type(t, b):
                return t[:, bass.ds(B * b, B), :].unsqueeze(3).broadcast_to((P, B, R, H))

            PER_B = 2

            def logits_batch(b, j):
                c = Chain("dve_b", PER_B * b)
                dve.wait_ge(s["kq0"] if j == 0 else s["kq1"], 16 * B * (b - j) + 32 * B)
                c.link(V.tensor_tensor(prod[:, j, :, :], kg[:, j, :, 0:HID], qg[:, j, :, :], ALU.mult))
                c.link(V.tensor_reduce(lsum[:, j, :, :], prod[:, j, :, :].rearrange("p b (h d) -> p b h d", h=H), AX_X, ALU.add))
                V.tensor_tensor(logit[:, bass.ds(B * b, B), :], lsum[:, j, :, :], kg[:, j, :, HID:KW], ALU.add).then_inc(s["logit_done"], 1)
                dve.wait_ge(s["tmax_mm"], upto(b - 2))
                dve.wait_ge(s["logit_done"], upto(b))
                V.tensor_tensor(ml[:, j, :, :, :], logit[:, bass.ds(B * b, B), :].unsqueeze(2).broadcast_to((P, B, R, H)),
                                per_type(tpen, b), ALU.add).then_inc(s["ml_ready"], 1)
                one_hots(b, j, s["oh_ready"])
                assert c.n == PER_B

            def scan(b, j):
                dve.wait_ge(s["f_ready"], upto(b - 1))
                dve.wait_ge(s["fb_ready"], upto(b - 2))
                dve.wait_ge(s["pen0"] if j == 0 else s["pen1"], 8 * (b - j) + 16)
                dve.wait_ge(s["mlt_ready"], upto(b))
                V.tensor_tensor_scan(fwd[:, j, :], pen_s[:, j, :], ml_ps[j][0:RH, :], fwd[:, 1 - j, B * P - 1:B * P],
                                     ALU.add, ALU.max).then_inc(s["f_ready"], 1)

            def take_window(b, nodes, window, summed, taken):
                at = dve.value_load(acc_row[0:1, bass.ds(b, 1)], min_val=0, max_val=(TILES - 1) * RH)
                dve.wait_ge(taken, upto(b - 1))
                dve.sem_inc(s["dve_turn"], 1)
                dve.wait_ge(summed, upto(b - 1))
                dve.sem_inc(s["dve_turn"], 1)
                V.tensor_tensor(nodes[:, bass.ds(at, WIN)], nodes[:, bass.ds(at, WIN)], window, ALU.add).then_inc(taken, 1)

            def pick_type(c, b, sel, src_bank, parts, tsel, expanded, taken):
                dve.wait_ge(expanded, upto(b))
                c.link(V.tensor_tensor(sel, src_bank[:, 0:parts * B * RH].rearrange("p (g n) -> p g n", n=parts * H),
                                       tmask[:].rearrange("p s r -> p (s r)")[:, bass.ds(B * R * b, B * R)].unsqueeze(2).broadcast_to((P, B * R, parts * H)),
                                       ALU.mult))
                dve.sem_inc(taken, 1)
                c.link(V.tensor_reduce(tsel, sel.rearrange("p (b r) (n h) -> p b h (r n)", b=B, h=H), AX_X, ALU.add))

            PER_C = 3

            def shifted_logits(b, j):
                c = Chain("dve_c", PER_C * b)
                pick_type(c, b, sel[:, j, :, :], exp_ps, 1, tsel[:, j, :, :], s["c_ex"], s["c_sel"])
                c.link(V.tensor_tensor(zed[:, j, :, :], logit[:, bass.ds(B * b, B), :], tsel[:, j, :, :], ALU.subtract))
                V.tensor_scalar(zed[:, j, :, :], zed[:, j, :, :], 0.0, None, ALU.min).then_inc(s["c_z"], 1)
                assert c.n == PER_C

            def exponentials_by_type(b, j):
                dve.wait_ge(s["c_den"], upto(b - 2))
                dve.wait_ge(s["c_p"], upto(b))
                V.tensor_tensor(pm[:, j, :, :, :], prob[:, bass.ds(B * b, B), :].unsqueeze(2).broadcast_to((P, B, R, H)),
                                per_type(tmask, b), ALU.mult).then_inc(s["c_pm"], 1)

            def take_max(b):
                take_window(b, node_max, win_t, s["tmax_mm"], s["t_acc"])

            def take_sum(b):
                take_window(b, node_sum, win_d, s["c_den"], s["d_acc"])

            def next_one_hots(b, j):
                dve.wait_ge(s["c_den"], upto(b - 1))
                one_hots(b + 1, 3 - j, s["c_oh"])

            def both_batches(b, j):
                logits_batch(b, j)
                shifted_logits(b - LAG, j)
                scan(b, j)
                next_one_hots(b - LAG, j)
                exponentials_by_type(b - LAG, j)
                take_max(b)
                take_sum(b - LAG)

            def logits_only(b, j):
                logits_batch(b, j)
                scan(b, j)
                take_max(b)

            def softmax_only(b, j):
                shifted_logits(b, j)
                next_one_hots(b, j)
                exponentials_by_type(b, j)
                take_sum(b)

            pairs(dve, 0, LAG, logits_only)
            dve.wait_ge(s["v_out"], TILES)
            V.memset(win_d, 0.0).then_inc(s["win_zero"], 1)
            V.memset(x_n[:, TILES - 1, :], 0.0).then_inc(s["x_room"], 1)
            dve.wait_ge(s["win_zero"], 3)
            dve.wait_ge(s["long_rdy"], 1)
            with dve.If(short_of(dve) > 0):
                one_hots(0, 2, s["c_oh"])
                pairs(dve, LAG, NB, both_batches)
                take_max(NB)
            with dve.If(long_of(dve) > 0):
                pairs(dve, LAG, NB, logits_only)
                take_max(NB)
                one_hots(0, 2, s["c_oh"])
                pairs(dve, 0, NB - LAG, softmax_only)

            def sums_with_x(t):
                at = bass.ds(t, 1)
                V.tensor_tensor(x_beta[:, at, :], x_n[:, at, :], be_all[:].unsqueeze(1), ALU.add)
                V.tensor_tensor(x_n[:, at, :], x_n[:, at, :], ob_all[:].unsqueeze(1), ALU.add).then_inc(s["x_sums"], 1)

            def softmax_end(b, q):
                shifted_logits(b, q % 2)
                dve.wait_ge(s["c_den"], upto(b - 2))
                one_hots(b + 2, end_slot(q + 2), s["c_oh"])
                exponentials_by_type(b, q % 2)
                sums_with_x(b - (NB - LAG))
                take_sum(b)

            one_hots(NB - LAG + 1, end_slot(1), s["c_oh"])
            dve.wait_ge(s["s_x"], 32)
            dve.wait_ge(s["s_vecs"], 48)
            sums_with_x(TILES - 1)
            fours(dve, softmax_end)
            shifted_logits(NB - 2, 0)
            exponentials_by_type(NB - 2, 0)
            take_sum(NB - 2)
            shifted_logits(NB - 1, 1)
            exponentials_by_type(NB - 1, 1)
            take_sum(NB - 1)
            take_sum(NB)
            c = Chain("split")
            sums = node_sum[:, 0:TILES * RH].rearrange("p (g h) -> p g h", h=H)
            dve.wait_ge(s["d_acc"], upto(NB))
            for n in range(2):
                c.link(V.tensor_copy(node3[:, :, n, :], sums))
                c.link(V.tensor_tensor(sums, sums, node3[:, :, n, :], ALU.subtract))
            c.link(V.tensor_copy(node3[:, :, 2, :], sums))
            V.tensor_scalar(neg_dloc[:], dloc[:], -1.0, None, ALU.mult).then_inc(s["nd_rdy"], 1)
            V.memset(psum[:, 0:7 * 512], 0.0).then_inc(s["nden_rdy"], 1)

            PER_D = 5

            def value_batch(b, j, values, arrived, landed):
                c = Chain("dve_d", PER_D * b)
                pick_type(c, b, sel3[:, j, :, :], bank[7], 3, tsel[:, j, :, :], s["d_ex"], s["d_sel"])
                c.link(V.tensor_scalar(tsel[:, j, :, :], tsel[:, j, :, :], 1e-12, None, ALU.add))
                c.link(V.reciprocal(tsel[:, j, :, :], tsel[:, j, :, :]))
                c.link(V.tensor_tensor(att[:, j, :, :], prob[:, bass.ds(B * b, B), :], tsel[:, j, :, :], ALU.mult))
                dve.wait_ge(s["v_mm"], upto(b - 2))
                dve.wait_ge(arrived, landed)
                V.tensor_tensor(prod[:, j, :, :].rearrange("p b (h d) -> p (b h) d", h=H), values.rearrange("p b (h d) -> p (b h) d", h=H),
                                att[:, j, :, :].rearrange("p b h -> p (b h)").unsqueeze(2).broadcast_to((P, B * H, D)), ALU.mult).then_inc(s["wv_ready"], 1)
                assert c.n == PER_D

            with dve.Fori(0, NB // 8) as i:
                for q, slot in enumerate(V_SLOT):
                    landed = 2 * i + 1 + q // 4 if slot < 3 else i + 1
                    value_batch(8 * i + q, q % 2, vg[:, slot, :, :], s[f"v{slot}"], landed * (16 * B))
                value_batch(8 * i + 7, 1, v_ahead[:, bass.ds(i, 1), :, :].rearrange("p a b c -> p (a b) c"), s["v_ahead"], 16 * B * (NB // 8))

            dve.wait_ge(s["v_mm"], upto(NB - 1))
            V.tensor_copy(agg[:].rearrange("p t c -> p (t c)")[:, 0:512 * HALF_G], agg_ps[:, 0:512 * HALF_G]).then_inc(s["agg_rdy"], 1)
            c = Chain("dve_t")
            dve.wait_ge(s["x_sums"], TILES)
            NG = len(GROUPS)

            def counted(ins):
                c.n += 1
                ins.then_inc(c.sem, 1)
                return c.n

            def standard_error(n):
                dve.wait_ge(s["var_rdy"], (n + 1) * NG)
                c.link(V.tensor_scalar(rstd[:, n, :], rstd[:, n, :], 1.0 / HID, 1e-5, ALU.mult, ALU.add))
                dve.sem_inc(s["sq_ask"], 1)
                dve.wait_ge(s["sq_got"], n + 1)
                c.link(V.reciprocal(rstd[:, n, :], rstd[:, n, :]))

            def of(g):
                return slice(GROUPS[g][0], GROUPS[g][-1] + 1)

            def group_of(v, g):
                return v.unsqueeze(1).broadcast_to((P, len(GROUPS[g]), HID))

            for g in range(NG):
                dve.wait_ge(s["o_mm"], g + 1)
                c.link(V.tensor_reduce(neg_mu[:, 0, of(g)], bank[g][:, 0:P * len(GROUPS[g])].rearrange("p (t c) -> p t c", c=HID), AX_X, ALU.add))
                V.tensor_scalar(neg_mu[:, 0, of(g)], neg_mu[:, 0, of(g)], -1.0 / HID, None, ALU.mult).then_inc(s["mu_rdy"], 1)
            dve.wait_ge(s["mu_rdy"], NG)
            standard_error(0)
            scaled, added = {}, {}
            for i in range(NG + 3):
                if i < NG:
                    for k, tile in enumerate(GROUPS[i]):
                        n = counted(V.tensor_scalar(hh[:, tile, :], bank[i][:, k * P:(k + 1) * P], neg_mu[:, 0, tile:tile + 1], rstd[:, 0, tile:tile + 1], ALU.add, ALU.mult))
                    scaled[i] = n
                g = i - 1
                if 0 <= g < NG:
                    dve.wait_ge(c.sem, scaled[g])
                    scaled[g] = counted(V.tensor_tensor(hh[:, of(g), :], hh[:, of(g), :], group_of(ga_all[:], g), ALU.mult))
                g = i - 2
                if 0 <= g < NG:
                    dve.wait_ge(c.sem, scaled[g])
                    added[g] = counted(V.tensor_tensor(hh[:, of(g), :], hh[:, of(g), :], x_beta[:, of(g), :], ALU.add))
                g = i - 3
                if 0 <= g < NG:
                    dve.wait_ge(c.sem, added[g])
                    c.link(V.tensor_reduce(neg_mu[:, 1, of(g)], hh[:, of(g), :], AX_X, ALU.add))
                    V.tensor_scalar(neg_mu[:, 1, of(g)], neg_mu[:, 1, of(g)], -1.0 / HID, None, ALU.mult).then_inc(s["mu_rdy"], 1)
            dve.wait_ge(s["mu_rdy"], 2 * NG)
            standard_error(1)
            for tiles in GROUPS:
                for tile in tiles:
                    last = V.tensor_scalar(sq[:, tile, :], hh[:, tile, :], neg_mu[:, 1, tile:tile + 1], rstd[:, 1, tile:tile + 1], ALU.add, ALU.mult)
                last.then_inc(s["fin"], 1)


INPUTS = ["x", "src", "dst", "edge_type_5", "L0_gnn_W_Q", "L0_gnn_W_K", "L0_gnn_W_V", "L0_gnn_attn_bias",
          "L0_gnn_out_proj_w", "L0_gnn_out_proj_b", "L0_gnn_ln_gamma", "L0_gnn_ln_beta"]


def kernel(**inputs):
    import numpy as np
    import concourse.bacc as bacc
    from concourse.bass_utils import run_bass_kernel_spmd

    nc = bacc.Bacc("TRN2", target_bir_lowering=False, num_devices=1)
    arrays, args = {}, []
    for name in INPUTS:
        a = np.ascontiguousarray(inputs[name])
        arrays[f"in_{name}_dram"] = a
        args.append(nc.dram_tensor(f"in_{name}_dram", a.shape, mybir.dt.from_np(a.dtype), kind="ExternalInput").ap())
    out = nc.dram_tensor("out_0_dram", inputs["x"].shape, F32, kind="ExternalOutput").ap()
    gnn_layer(nc, *args, out)
    r = run_bass_kernel_spmd(nc, [arrays], core_ids=[0])
    return r.results[0]["out_0_dram"]
```
